# Optimizing a Trainium2 kernel written in Bass

```python
import numpy as np
import jax
import jax.numpy as jnp

def _softmax(x, axis=-1):
    return jax.nn.softmax(x, axis=axis)

def _gelu(x):
    return jax.nn.gelu(x, approximate=True)

def _silu(x):
    return jax.nn.silu(x)

def _sigmoid(x):
    return jax.nn.sigmoid(x)

def _layernorm(x, axis=-1, eps=1e-05):
    m = jnp.mean(x, axis=axis, keepdims=True)
    v = jnp.var(x, axis=axis, keepdims=True)
    return (x - m) / jnp.sqrt(v + eps)

def _scatter_add(tgt, idx, src, axis=0):
    return tgt.at[idx].add(src)

def _segment_sum(src, seg, n):
    return jax.ops.segment_sum(src, seg, n)
kernel_name = 'mk_gnn_preln_d1_gnn_r32_750afc'

def setup_inputs(seed: int=0):
    np.random.seed(seed)
    _w = jnp.asarray

    def _rec_inputs():
        import jax
        import jax.numpy as jnp
        _gk = jax.random.key(seed)
        x = 0.009969 + 0.2191 * jax.random.normal(jax.random.fold_in(_gk, 1), (3125, 256), jnp.float32)
        _s = jax.random.randint(jax.random.fold_in(_gk, 2), (25000,), 0, 3125, jnp.int32)
        _d = jax.random.randint(jax.random.fold_in(_gk, 3), (25000,), 0, 3125, jnp.int32)
        _loop = jnp.arange(3125, dtype=jnp.int32)
        src = jnp.concatenate([_s, _d, _loop])
        dst = jnp.concatenate([_d, _s, _loop])
        _o = jnp.argsort(dst, stable=True)
        src = src[_o]
        dst = dst[_o]
        edge_weight1 = jax.random.uniform(jax.random.fold_in(_gk, 12), (53125, 1), jnp.float32, 0.0, 1)
        node_vec1 = jax.random.uniform(jax.random.fold_in(_gk, 13), (3125, 1), jnp.float32, 0.0, 1)
        return (x, src, dst, edge_weight1, node_vec1)
    x, src, dst, edge_weight1, node_vec1 = _rec_inputs()

    def _L0_gnn_setup():
        import jax, jax.numpy as jnp
        import numpy as np
        C = 1.0
        K = 1.0 / C
        SQRTK = K ** 0.5
        EPS = 1e-07
        MIN_NORM = 1e-15
        MAX_NORM = 1000000.0
        NORM_FACTOR = 100.0

        def mink_dot(x, y):
            return -x[..., 0:1] * y[..., 0:1] + jnp.sum(x[..., 1:] * y[..., 1:], axis=-1, keepdims=True)

        def mink_norm(u):
            return jnp.sqrt(jnp.clip(mink_dot(u, u), EPS, None))

        def arcosh(t):
            return jnp.arccosh(jnp.clip(t, 1.0 + EPS, None))

        def proj(x):
            y = x[..., 1:]
            x0 = jnp.sqrt(K + jnp.sum(y * y, axis=-1, keepdims=True))
            return jnp.concatenate([x0, y], axis=-1)

        def proj_tan(u, x):
            ux = jnp.sum(x[..., 1:] * u[..., 1:], axis=-1, keepdims=True)
            u0 = ux / jnp.clip(x[..., 0:1], EPS, None)
            return jnp.concatenate([u0, u[..., 1:]], axis=-1)

        def expmap(u, x):
            normu = jnp.clip(mink_norm(u), None, MAX_NORM)
            theta = jnp.clip(normu / SQRTK, MIN_NORM, None)
            return proj(jnp.cosh(theta) * x + jnp.sinh(theta) * u / theta)

        def sqdist(x, y):
            theta = jnp.clip(-mink_dot(x, y) / K, 1.0 + EPS, None)
            return jnp.clip(K * arcosh(theta) ** 2, None, 50.0)

        def logmap(x, y):
            xy = jnp.clip(mink_dot(x, y) + K, None, -EPS) - K
            u = y + xy * x * C
            normu = jnp.clip(mink_norm(u), MIN_NORM, None)
            dist = jnp.sqrt(sqdist(x, y))
            return proj_tan(dist * u / normu, x)

        def logmap0(x):
            y = x[..., 1:]
            y_norm = jnp.clip(jnp.linalg.norm(y, axis=-1, keepdims=True), MIN_NORM, None)
            theta = jnp.clip(x[..., 0:1] / SQRTK, 1.0 + EPS, None)
            res = SQRTK * arcosh(theta) * y / y_norm
            return jnp.concatenate([jnp.zeros_like(x[..., 0:1]), res], axis=-1)

        def expmap0(u):
            y = u[..., 1:]
            y_norm = jnp.clip(jnp.linalg.norm(y, axis=-1, keepdims=True), MIN_NORM, None)
            theta = y_norm / SQRTK
            return proj(jnp.concatenate([SQRTK * jnp.cosh(theta), SQRTK * jnp.sinh(theta) * y / y_norm], axis=-1))
        N, E, D, EDGE_DIM = (10000, 10000, 256, 1)
        key = jax.random.key(seed)
        ks = jax.random.split(key, 12)
        u = jnp.concatenate([jnp.zeros((N, 1), jnp.float32), 0.1 * jax.random.normal(ks[0], (N, D - 1), jnp.float32)], axis=-1)
        x = expmap0(u)
        distances = jax.random.uniform(ks[1], (E, EDGE_DIM), jnp.float32)
        edges = jax.random.randint(ks[2], (2, E), 0, N)
        node_mask = jnp.ones((N, 1), jnp.float32)
        edge_mask = jnp.ones((E, 1), jnp.float32)
        s = 0.02
        return {'x': x, 'distances': distances, 'edges': edges, 'node_mask': node_mask, 'edge_mask': edge_mask, 'att_w1': s * jax.random.normal(ks[3], (2 * D + EDGE_DIM, D), jnp.float32), 'att_b1': jnp.zeros((D,), jnp.float32), 'att_w2': s * jax.random.normal(ks[4], (D, 1), jnp.float32), 'att_b2': jnp.zeros((1,), jnp.float32), 'mlp_w1': s * jax.random.normal(ks[5], (D, D), jnp.float32), 'mlp_b1': jnp.zeros((D,), jnp.float32), 'mlp_w2': s * jax.random.normal(ks[6], (D, D), jnp.float32), 'mlp_b2': jnp.zeros((D,), jnp.float32)}
    _L0_gnn_all = _L0_gnn_setup()
    _L0_gnn_in = {k: v for k, v in _L0_gnn_all.items() if k in ('att_w1', 'att_b1', 'att_w2', 'att_b2', 'mlp_w1', 'mlp_b1', 'mlp_w2', 'mlp_b2')}
    del _L0_gnn_all
    return {'x': x, 'src': src, 'dst': dst, 'edge_weight1': edge_weight1, 'node_vec1': node_vec1, 'L0_gnn_att_w1': _L0_gnn_in['att_w1'], 'L0_gnn_att_b1': _L0_gnn_in['att_b1'], 'L0_gnn_att_w2': _L0_gnn_in['att_w2'], 'L0_gnn_att_b2': _L0_gnn_in['att_b2'], 'L0_gnn_mlp_w1': _L0_gnn_in['mlp_w1'], 'L0_gnn_mlp_b1': _L0_gnn_in['mlp_b1'], 'L0_gnn_mlp_w2': _L0_gnn_in['mlp_w2'], 'L0_gnn_mlp_b2': _L0_gnn_in['mlp_b2']}

def reference(x, src, dst, edge_weight1, node_vec1, L0_gnn_att_w1, L0_gnn_att_b1, L0_gnn_att_w2, L0_gnn_att_b2, L0_gnn_mlp_w1, L0_gnn_mlp_b1, L0_gnn_mlp_w2, L0_gnn_mlp_b2):
    import jax
    import jax.numpy as jnp

    def _L0_gnn_ref(x, distances, edges, node_mask, edge_mask, att_w1, att_b1, att_w2, att_b2, mlp_w1, mlp_b1, mlp_w2, mlp_b2):
        import jax, jax.numpy as jnp
        import numpy as np
        C = 1.0
        K = 1.0 / C
        SQRTK = K ** 0.5
        EPS = 1e-07
        MIN_NORM = 1e-15
        MAX_NORM = 1000000.0
        NORM_FACTOR = 100.0

        def mink_dot(x, y):
            return -x[..., 0:1] * y[..., 0:1] + jnp.sum(x[..., 1:] * y[..., 1:], axis=-1, keepdims=True)

        def mink_norm(u):
            return jnp.sqrt(jnp.clip(mink_dot(u, u), EPS, None))

        def arcosh(t):
            return jnp.arccosh(jnp.clip(t, 1.0 + EPS, None))

        def proj(x):
            y = x[..., 1:]
            x0 = jnp.sqrt(K + jnp.sum(y * y, axis=-1, keepdims=True))
            return jnp.concatenate([x0, y], axis=-1)

        def proj_tan(u, x):
            ux = jnp.sum(x[..., 1:] * u[..., 1:], axis=-1, keepdims=True)
            u0 = ux / jnp.clip(x[..., 0:1], EPS, None)
            return jnp.concatenate([u0, u[..., 1:]], axis=-1)

        def expmap(u, x):
            normu = jnp.clip(mink_norm(u), None, MAX_NORM)
            theta = jnp.clip(normu / SQRTK, MIN_NORM, None)
            return proj(jnp.cosh(theta) * x + jnp.sinh(theta) * u / theta)

        def sqdist(x, y):
            theta = jnp.clip(-mink_dot(x, y) / K, 1.0 + EPS, None)
            return jnp.clip(K * arcosh(theta) ** 2, None, 50.0)

        def logmap(x, y):
            xy = jnp.clip(mink_dot(x, y) + K, None, -EPS) - K
            u = y + xy * x * C
            normu = jnp.clip(mink_norm(u), MIN_NORM, None)
            dist = jnp.sqrt(sqdist(x, y))
            return proj_tan(dist * u / normu, x)

        def logmap0(x):
            y = x[..., 1:]
            y_norm = jnp.clip(jnp.linalg.norm(y, axis=-1, keepdims=True), MIN_NORM, None)
            theta = jnp.clip(x[..., 0:1] / SQRTK, 1.0 + EPS, None)
            res = SQRTK * arcosh(theta) * y / y_norm
            return jnp.concatenate([jnp.zeros_like(x[..., 0:1]), res], axis=-1)

        def expmap0(u):
            y = u[..., 1:]
            y_norm = jnp.clip(jnp.linalg.norm(y, axis=-1, keepdims=True), MIN_NORM, None)
            theta = y_norm / SQRTK
            return proj(jnp.concatenate([SQRTK * jnp.cosh(theta), SQRTK * jnp.sinh(theta) * y / y_norm], axis=-1))
        row, col = (edges[0], edges[1])
        N = x.shape[0]
        x_tangent = logmap0(x)
        x_local_tangent = logmap(x[row], x[col])
        x_local_self_tangent = logmap(x, x)
        cat = jnp.concatenate([x_tangent[row], x_tangent[col], distances], axis=-1)
        h = jax.nn.silu(cat @ att_w1 + att_b1)
        att = jax.nn.sigmoid(h @ att_w2 + att_b2) * edge_mask
        agg = jax.ops.segment_sum(x_local_tangent * att, row, num_segments=N) / NORM_FACTOR
        mlp_out = jax.nn.silu(agg @ mlp_w1 + mlp_b1) @ mlp_w2 + mlp_b2
        out = x_local_self_tangent + mlp_out
        support_t = proj_tan(out, x)
        return expmap(support_t, x)
    edge_index = jnp.stack([src, dst])
    h = jnp.maximum(_layernorm(x, axis=-1), 0.0)
    x = x + _L0_gnn_ref(h, edge_weight1, edge_index, node_vec1, edge_weight1, L0_gnn_att_w1, L0_gnn_att_b1, L0_gnn_att_w2, L0_gnn_att_b2, L0_gnn_mlp_w1, L0_gnn_mlp_b1, L0_gnn_mlp_w2, L0_gnn_mlp_b2)
    return x

_drawn_inputs = setup_inputs


def setup_inputs(seed=0):
    import zlib

    import numpy as np

    out = dict(_drawn_inputs(seed))
    spreads = {'L0_gnn_att_b1': (0.0, 0.8), 'L0_gnn_mlp_b1': (0.0, 0.334), 'L0_gnn_mlp_b2': (0.0, 0.1)}
    factors = {'L0_gnn_att_w1': 40.091, 'L0_gnn_att_w2': 8.0}
    for name, (base, spread) in spreads.items():
        noise = np.random.default_rng([zlib.crc32(name.encode()), seed]).standard_normal(out[name].shape)
        drawn = base * np.exp(spread * noise) if base else spread * noise
        out[name] = jnp.asarray(drawn.astype(out[name].dtype))
    for name, factor in factors.items():
        out[name] = (out[name] * factor).astype(out[name].dtype)
    return out
```

```python
import concourse.bass as bass
from concourse import mybir
from contextlib import ExitStack


def hyperbolic_gnn_layer(nc, x, src, dst, dist, att_w1, att_b1, att_w2, att_b2,
                         mlp_w1, mlp_b1, mlp_w2, mlp_b2, out):
    fp32 = mybir.dt.float32
    bf16 = mybir.dt.bfloat16
    i32 = mybir.dt.int32
    ALU = mybir.AluOpType
    ACT = mybir.ActivationFunctionType
    AX = mybir.AxisListType

    N, D = x.shape
    E = src.shape[0]
    P = 128
    NP = 125
    NB = N // NP
    EC = E // NP
    PAIR = 2 * P
    TG = 16
    PG = TG // 2
    HT = TG // 2
    NPAIR = (E + NB * (PAIR - 1)) // PAIR
    NG = -(-NPAIR // PG)
    assert NB * NP == N and EC * NP == E and NG % 2 == 1
    NPAIR = NG * PG
    J = 2 * NPAIR
    EPS = 1e-7
    SELF_MAX = -1.0000001
    MAGIC = 12582912.0
    NQ = -(-NB // 4)
    CHAIN = 13
    CHAIN_A = 6
    LATE = 5

    sorted_dram = nc.dram_tensor("sorted_edges", (P * J, 4), fp32).ap()
    node_dram = nc.dram_tensor("node_rows", (N, 2 * D), fp32).ap()

    ctx = ExitStack()
    with ctx:
        def sb(name, shape, dt=fp32):
            return ctx.enter_context(nc.sbuf_tensor(name, shape, dt))

        def pb(name, shape, dt=fp32):
            return ctx.enter_context(nc.psum_tensor(name, shape, dt))

        def sem(name):
            return ctx.enter_context(nc.semaphore(name))

        parts = [sb(f"node_part{k}", [P, NB, 2 * D], bf16) for k in range(3)]
        sums = sb("sums", [P, NB, D])
        gathered = sb("gathered", [P, 2, HT, 2 * D])
        tangents = sb("tangents", [P, 2, TG, D])
        recs = sb("recs", [P, J + 4, 4])
        dist_parts = sb("dist_parts", [P, J + 4, 3], bf16)
        onehot = sb("onehot", [P, TG, P], bf16)
        onehot_t = sb("onehot_t", [P, 2, 2, P], bf16)
        weighted = sb("weighted", [P, 2, 2, P])
        hidden = sb("hidden", [P, 2, 2, D])
        dot_out = sb("dot_out", [P, 2, D])
        mink_out = sb("mink_out", [P, 2, D])
        square_out = sb("square_out", [P, 2, D])
        ident = sb("ident", [P, P])
        ident_b = sb("ident_b", [P, P], bf16)
        iota_f = sb("iota_f", [P, P])
        iota_b = sb("iota_b", [P, P], bf16)
        ones = sb("ones", [P, P])
        before = sb("before", [P, P])
        w1c = sb("w1c", [P, D])
        b1row = sb("b1row", [P, D])
        w2row = sb("w2row", [P, D])
        mb2row = sb("mb2row", [P, D])
        mb1col = sb("mb1col", [P, 2])
        b2col = sb("b2col", [P, 1])
        nb2col = sb("nb2col", [P, 1])
        idx_now = sb("idx_now", [P, 2, HT], i32)
        bucket_of = sb("bucket_of", [1, NPAIR], i32)
        neg0 = sb("neg0", [P, 2, 2])
        mink = sb("mink", [P, TG])
        xy = sb("xy", [P, 2, TG])
        uu = sb("uu", [P, 2, TG])
        logit = sb("logit", [P, 2, TG])
        wt = [sb(f"wt{k}", [P, TG]) for k in range(14)]
        weight = sb("weight", [P, 2, TG])
        small = sb("small", [P, 24, NB])
        counts = sb("counts", [P, NB])
        off = sb("off", [P, 5, NB])
        stats = sb("stats", [P, 2, 6])
        meanvar = sb("meanvar", [P, NB, 2])

        sort = sums[:, :, :].rearrange("p b d -> p (b d)")

        def col(k):
            return sort[0:NP, k * EC:(k + 1) * EC]

        src_i = col(0).bitcast(i32)
        dst_i = col(1).bitcast(i32)
        dist_in = col(2)
        src_f, buck, local, pos, ind, scan, tmp = (col(k) for k in range(3, 10))
        pos_i, lo_i, hi_i, row_i = (col(k).bitcast(i32) for k in (0, 7, 8, 1))
        ones_row = col(14)
        rec_src = sort[0:NP, 10 * EC:14 * EC].rearrange("p (t c) -> p t c", c=4)
        xin = tangents[0:NP, :, :, :].rearrange("p a t d -> p (a t) d")[:, 0:NB, :]
        w1 = tangents[:, :, :, :].rearrange("p a t d -> p (a t d)")[:, NB * D:NB * D + 4 * D] \
            .rearrange("p (c d) -> p c d", c=2)
        h = gathered[0:NP, :, :, :].rearrange("p a t d -> p (a t d)")[:, 0:NB * D] \
            .rearrange("p (b d) -> p b d", d=D)
        hT = hidden[:, :, :, :].rearrange("p a i d -> p a (i d)")
        pf = dot_out
        rest = mink_out
        SC = 17
        rest_d = mink_out[:, :, :].rearrange("p a d -> p (a d)")[:, 0:J + 4]
        w1c_parts = sb("w1c_parts", [P, 3, D], bf16)
        pair_iota = sb("pair_iota", [1, NPAIR])
        pair_acc = sb("pair_acc", [1, NPAIR])
        slot_idx = sb("slot_idx", [P, 2, SC], i32)
        slot_rec = sb("slot_rec", [P, 2, SC, 4])

        def quad_buffers(k):
            flat = parts[k][:, :, :].rearrange("p b d -> p (b d)").bitcast(fp32)
            return [flat[:, i * 1024:(i + 1) * 1024].rearrange("p (c n) -> p c n", c=2) for i in range(2)]

        sumT, hidT = quad_buffers(0), quad_buffers(1)

        mw1, mw2 = (parts[2][:, 4 * k:4 * k + 2, :].rearrange("p b d -> p (b d)").bitcast(fp32)
                    .rearrange("p (c d) -> p c d", c=2)[:, :, 0:D] for k in range(2))

        def quad(q):
            return range(4 * q, min(NB, 4 * q + 4))

        h_ps, z_ps, turn_ps, agg_ps = ([pb(f"{name}_ps{k}", [P, 2 * D]) for k in range(2)]
                                       for name in ("h", "z", "turn", "agg"))
        at_ps = [t[:, 0:P].bitcast(bf16) for t in turn_ps]

        def two(bank):
            return bank[:, :].rearrange("p (k d) -> p k d", k=2)

        s = {}
        for name in (
                "edges_in", "weights_in", "x_in", "mlp_in",
                "consts_ready", "pool_step", "pool_turn", "defaults", "w1_zeroed", "w1c_split", "table_tails",
                "fill_out", "vec", "counted", "count_ps", "sort_done", "slot_filled",
                "scattered0", "scattered1", "recs_in", "base_done",
                "var_ready", "std_ready", "h_ready", "sq_setup", "theta_ready", "root_ready",
                "log_arg", "log_ready", "coef_ready", "ht_ps", "ht_sb", "pq_ps", "pf_ready",
                "part0", "rest_ready", "part1", "part2", "q_ready", "h_out", "q_out",
                "buckets_ready", "idx_ready", "gath0", "gath1", "onehots", "at_ready",
                "at_copied", "expanded", "silu_done", "neg_done", "mink_done", "xy_done",
                "u_ready", "sq_done", "dot_done", "w_vec", "w_act", "weighted_ready",
                "agg_summed", "agg_added", "h_back", "x_back", "tail_agg", "self_u", "self_sq",
                "tail_ask", "tail_say", "t_ps", "t_sb", "m1_ps", "m1_sb", "m2_ps", "m2_sb",
                "o_ready", "o_sq", "y_ready", "y_sq", "out_ready", "out_done"):
            s[name] = sem(name)

        def wait(eng, name, value):
            if not (isinstance(value, int) and value <= 0):
                eng.wait_ge(s[name], value)

        block = ctx.enter_context(nc.Block())

        def groups(eng, first, body, last):
            first((0, 0))
            with eng.Fori(0, (NG - 1) // 2) as i:
                body((i, 1))
                body((i, 2))
            last((0, NG - 1))

        def at(g, per, plus):
            i, o = g
            return per * o + plus if isinstance(i, int) else i * (2 * per) + (per * o + plus)

        def back(g, n=1):
            return (g[0], g[1] - n)

        @block.sync
        def _(sp):
            for a, d in ((src, src_i), (dst, dst_i), (dist, dist_in)):
                sp.dma_start(d, a.rearrange("(p t) -> p t", p=NP)).then_inc(s["edges_in"], 16)
            sp.dma_start(xin, x.rearrange("(b l) d -> l b d", l=NP)).then_inc(s["x_in"], 16)
            for half in range(2):
                sp.dma_start(w1[:, :, half * D:(half + 1) * D],
                             att_w1[half * D:(half + 1) * D, :].rearrange("(c p) d -> p c d", p=P)) \
                    .then_inc(s["weights_in"], 16)
            for a, d in ((att_w1[2 * D:2 * D + 1, :], w1c), (att_b1[None, :], b1row),
                         (att_w2.rearrange("d o -> o d"), w2row), (mlp_b2[None, :], mb2row)):
                sp.dma_start(d[:, :], a.broadcast_to((P, D))).then_inc(s["weights_in"], 16)
            for c in range(2):
                sp.dma_start(mb1col[:, c:c + 1], mlp_b1[c * P:(c + 1) * P][:, None]).then_inc(s["weights_in"], 16)
            sp.dma_start(b2col[:, :], att_b2[None, :].broadcast_to((P, 1))).then_inc(s["weights_in"], 16)
            sp.wait_ge(s["defaults"], 1)
            sp.dma_start(sorted_dram.rearrange("(p j) c -> p (j c)", p=P),
                         recs[:, 0:J, :].rearrange("p j c -> p (j c)")).then_inc(s["fill_out"], 16)
            rows = node_dram.rearrange("(b l) d -> l b d", l=NP)
            sp.wait_ge(s["h_ready"], 1)
            sp.dma_start(rows[:, :, 0:D], h).then_inc(s["h_out"], 16)
            sp.wait_ge(s["q_ready"], NB)
            sp.dma_start(rows[:, :, D:2 * D], xin).then_inc(s["q_out"], 16)
            sp.wait_ge(s["scattered0"], 16 * SC * ((EC // SC + 1) // 2))
            sp.wait_ge(s["scattered1"], 16 * SC * (EC // SC // 2))
            sp.dma_start(recs[:, 0:J, :].rearrange("p j c -> p (j c)"),
                         sorted_dram.rearrange("(p j) c -> p (j c)", p=P)).then_inc(s["recs_in"], 16)
            sp.wait_ge(s["expanded"], NPAIR)
            sp.wait_ge(s["u_ready"], J)
            sp.dma_start(h, rows[:, :, 0:D]).then_inc(s["h_back"], 16)
            for a, d in ((mlp_w1, mw1), (mlp_w2, mw2)):
                sp.dma_start(d, a.rearrange("(c p) d -> p c d", p=P)).then_inc(s["mlp_in"], 16)
            sp.wait_ge(s["agg_summed"], NPAIR)
            sp.wait_ge(s["sq_done"], J)
            sp.dma_start(xin, x.rearrange("(b l) d -> l b d", l=NP)).then_inc(s["x_back"], 16)
            sp.wait_ge(s["out_ready"], 1)
            sp.dma_start(out.rearrange("(b l) d -> l b d", l=NP), xin).then_inc(s["out_done"], 16)
            sp.wait_ge(s["out_done"], 16)

        @block.gpsimd
        def _(pool):
            n = [0]

            def step(ins):
                n[0] += 1
                ins.then_inc(s["pool_step"], 1)
                pool.wait_ge(s["pool_step"], n[0])

            g = nc.gpsimd
            step(g.memset(recs[:, :, :], 0.0))
            step(g.memset(recs[:, :, 0:1], -1.0))
            pool.nop().then_inc(s["defaults"], 1)
            step(g.memset(ones[:, :], 1.0))
            step(g.affine_select(out=ident[:, :], in_=ones[:, :], compare_op=ALU.is_equal, fill=0.0, base=0,
                                 pattern=[[-1, P]], channel_multiplier=1))
            step(g.affine_select(out=before[:, :], in_=ones[:, :], compare_op=ALU.is_gt, fill=0.0, base=0,
                                 pattern=[[1, P]], channel_multiplier=-1))
            step(g.tensor_copy(ident_b[:, :], ident[:, :]))
            step(g.iota(pair_iota[:, :], pattern=[[1, NPAIR]], base=0, channel_multiplier=0,
                        allow_small_or_imprecise_dtypes=True))
            step(g.iota(iota_f[:, :], pattern=[[1, P]], base=0, channel_multiplier=0,
                        allow_small_or_imprecise_dtypes=True))
            step(g.tensor_copy(iota_b[:, :], iota_f[:, :]))
            pool.nop().then_inc(s["consts_ready"], 1)
            pool.wait_ge(s["weights_in"], 16 * 9)
            g.memset(w1[0:1, 0, :], 0.0).then_inc(s["w1_zeroed"], 1)
            for k in range(3):
                step(g.memset(parts[k][96:P, :, 0:D], 0.0))
            pool.wait_ge(s["w1c_split"], 1)
            for k in range(3):
                step(g.tensor_copy(parts[k][96:P, :, D:2 * D],
                                   w1c_parts[96:P, k, None, :].broadcast_to((32, NB, D))))
            pool.nop().then_inc(s["table_tails"], 1)

            pool.wait_ge(s["sort_done"], 1)
            pool.wait_ge(s["fill_out"], 16)

            def scatter(i, slot, first_use, count):
                base = i * (2 * SC) + slot * SC
                if not first_use:
                    pool.wait_ge(s[f"scattered{slot}"], count * (16 * SC))
                g.tensor_copy(slot_idx[0:NP, slot, :], row_i[:, bass.ds(base, SC)]).then_inc(s["slot_filled"], 1)
                g.tensor_copy(slot_rec[0:NP, slot, :, :], rec_src[:, bass.ds(base, SC), :]).then_inc(s["slot_filled"], 1)
                pool.wait_ge(s["slot_filled"], i * 4 + 2 * slot + 2)
                pool.nop().then_inc(s["pool_turn"], 1)
                for c in range(SC):
                    g.indirect_dma_start(sorted_dram,
                                         bass.IndirectOffsetOnAxis(ap=slot_idx[0:NP, slot, c:c + 1], axis=0),
                                         slot_rec[0:NP, slot, c, :], None).then_inc(s[f"scattered{slot}"], 16)

            steps = EC // SC
            scatter(0, 0, True, 0)
            scatter(0, 1, True, 0)
            with pool.Fori(1, steps // 2) as i:
                scatter(i, 0, False, i)
                scatter(i, 1, False, i)
            if steps % 2:
                scatter(steps // 2, 0, False, steps // 2)

            pool.wait_ge(s["recs_in"], 16)
            pool.wait_ge(s["h_out"], 16)
            pool.wait_ge(s["q_out"], 16)
            pool.wait_ge(s["part2"], NB)
            pool.wait_ge(s["sq_setup"], NB)
            dst_of = recs[:, :, 1].bitcast(i32)

            def gather(gr):
                for half in range(2):
                    wait(pool, "expanded", at(gr, PG, half * PG // 2 - PG // 2))
                    wait(pool, "u_ready", at(gr, TG, half * HT - HT))
                    wait(pool, f"gath{half}", at(gr, 16 * HT, 0))
                    g.tensor_copy(idx_now[:, half, :], dst_of[:, bass.ds(at(gr, TG, half * HT), HT)]) \
                        .then_inc(s["idx_ready"], 1)
                    pool.wait_ge(s["idx_ready"], at(gr, 2, half + 1))
                    pool.nop().then_inc(s["pool_turn"], 1)
                    for c in range(HT):
                        g.indirect_dma_start(gathered[:, half, c, :], None, node_dram,
                                             bass.IndirectOffsetOnAxis(ap=idx_now[:, half, c:c + 1], axis=0)) \
                            .then_inc(s[f"gath{half}"], 16)

            groups(pool, gather, gather, lambda gr: None)

        @block.tensor
        def _(pe):
            t = nc.tensor
            pe.wait_ge(s["consts_ready"], 1)
            pe.wait_ge(s["counted"], 1)
            t.matmul(agg_ps[0][0:NP, 0:NB], before[0:NP, 0:NP], counts[0:NP, :], start=True, stop=True)
            t.matmul(agg_ps[1][:, 0:NB], ones[0:NP, :], counts[0:NP, :], start=True, stop=True).then_inc(s["count_ps"], 1)
            pe.wait_ge(s["weights_in"], 16 * 9)
            pe.wait_ge(s["h_ready"], 1)
            pe.wait_ge(s["w1_zeroed"], 1)

            def turn(b):
                wait(pe, "ht_sb", b - 1)
                for c in range(2):
                    last = t.transpose(turn_ps[b % 2][:, c * NP:(c + 1) * NP], h[:, b, c * P:(c + 1) * P],
                                       ident[0:NP, 0:NP])
                last.then_inc(s["ht_ps"], 1)

            turn(0)
            for b in range(NB):
                if b + 1 < NB:
                    turn(b + 1)
                pe.wait_ge(s["ht_sb"], b + 1)
                wait(pe, "pf_ready", b - 1)
                wait(pe, "q_ready", b - 1)
                for bank, half in ((z_ps, 0), (h_ps, 1)):
                    for c in range(2):
                        last = t.matmul(bank[b % 2][0:NP, 0:D], hT[:, b % 2, c * NP:(c + 1) * NP],
                                        w1[:, c, half * D:(half + 1) * D], start=(c == 0), stop=(c == 1))
                last.then_inc(s["pq_ps"], 1)

            bucket = [t.alloc_register(f"pe_bucket{j}") for j in range(PG)]
            pe.wait_ge(s["buckets_ready"], 1)
            pe.wait_ge(s["part2"], NB)
            pe.wait_ge(s["table_tails"], 1)
            pe.wait_ge(s["sq_setup"], NB)

            def turn_onehots(gr, j):
                slot = j % 2
                wait(pe, "onehots", at(gr, 3 * PG, 3 * j + 3))
                wait(pe, "at_copied", at(gr, PG, j - 1))
                for k in range(2):
                    last = t.transpose(at_ps[slot][:, k * P:(k + 1) * P], onehot[:, 2 * j + k, :], ident_b[:, :])
                last.then_inc(s["at_ready"], 1)

            def expand(gr, j, b):
                slot = j % 2
                wait(pe, "at_copied", at(gr, PG, j + 1))
                wait(pe, f"gath{j // (PG // 2)}", at(gr, 16 * HT, 16 * HT))
                wait(pe, "u_ready", at(gr, TG, 2 * j - 2))
                wait(pe, "silu_done", at(gr, PG, j - 1))
                for k in range(2):
                    h_out, z_out = (bank[slot][:, k * D:(k + 1) * D] for bank in (h_ps, z_ps))
                    for part in range(3):
                        for o, half in ((h_out, 0), (z_out, 1)):
                            t.matmul(o, onehot_t[:, slot, k, :],
                                     parts[part][:, bass.ds(b, 1), half * D:(half + 1) * D],
                                     start=(part == 0), stop=(part == 2 and half == 0))
                    last = t.matmul(z_out, ident[:, :], gathered[:, j // (PG // 2), (2 * j + k) % HT, D:2 * D],
                                    start=False, stop=True)
                last.then_inc(s["expanded"], 1)

            def add_up(gr, j):
                slot = j % 2
                par = gr[1] % 2
                wait(pe, "weighted_ready", at(gr, TG, 2 * j + 2))
                wait(pe, "agg_added", at(gr, PG, j + 1))
                for k in range(2):
                    last = t.matmul(agg_ps[slot][0:NP, 0:D], weighted[:, slot, k, 0:NP],
                                    tangents[:, par, 2 * j + k, :], start=(k == 0), stop=(k == 1))
                last.then_inc(s["agg_summed"], 1)

            def pe_group(gr, sum_last=True):
                for j in range(PG):
                    t.reg_load(bucket[j], bucket_of[0:1, bass.ds(at(gr, PG, j), 1)])
                for j in range(PG):
                    if j + 1 < PG:
                        turn_onehots(gr, j + 1)
                    expand(gr, j, t.snap(bucket[j]))
                    if sum_last and j < LATE:
                        add_up(back(gr), j)
                turn_onehots(back(gr, -1), 0)
                if sum_last:
                    for j in range(LATE, PG):
                        add_up(back(gr), j)

            def pe_first(gr):
                turn_onehots(gr, 0)
                pe_group(gr, sum_last=False)

            def pe_last(gr):
                for j in range(PG):
                    add_up(gr, j)

            groups(pe, pe_first, pe_group, pe_last)

            pe.wait_ge(s["tail_agg"], 1)
            pe.wait_ge(s["mlp_in"], 32)

            def turn_sums(q):
                wait(pe, "t_sb", 2 * q)
                for c in range(2):
                    for n, b in enumerate(quad(q)):
                        last = t.transpose(turn_ps[c][:, n * NP:(n + 1) * NP], sums[0:NP, b, c * P:(c + 1) * P],
                                           ident[0:NP, 0:NP])
                last.then_inc(s["t_ps"], 1)

            turn_sums(0)
            for q in range(NQ):
                n_cols = len(quad(q)) * NP
                pe.wait_ge(s["t_sb"], 2 * q + 2)
                wait(pe, "m1_sb", 2 * q)
                for f in range(2):
                    for c in range(2):
                        last = t.matmul(z_ps[f][:, 0:n_cols], mw1[:, c, f * P:(f + 1) * P],
                                        sumT[q % 2][:, c, 0:n_cols], start=(c == 0), stop=(c == 1))
                    last.then_inc(s["m1_ps"], 1)
                if q + 1 < NQ:
                    turn_sums(q + 1)
                pe.wait_ge(s["m1_sb"], 2 * q + 2)
                for n, b in enumerate(quad(q)):
                    wait(pe, "m2_sb", b - 1)
                    for f in range(2):
                        last = t.matmul(agg_ps[b % 2][0:NP, 0:D], hidT[q % 2][:, f, n * NP:(n + 1) * NP],
                                        mw2[:, f, :], start=(f == 0), stop=(f == 1))
                    last.then_inc(s["m2_ps"], 1)

        @block.scalar
        def _(act):
            a = nc.scalar
            act.wait_ge(s["var_ready"], 1)
            a.activation(small[0:NP, 1, :], small[0:NP, 0, :], ACT.Sqrt).then_inc(s["std_ready"], 1)
            act.wait_ge(s["h_ready"], 1)
            act.wait_ge(s["base_done"], 1)
            for b in range(NB):
                wait(act, "sq_setup", b - 1)
                a.activation(square_out[0:NP, b % 2, 0:D - 1], h[:, b, 1:D], ACT.Square,
                             accum_out=small[0:NP, 2, b:b + 1]).then_inc(s["sq_setup"], 1)
            act.wait_ge(s["theta_ready"], 1)
            act.wait_ge(s["sq_setup"], NB)
            a.activation(small[0:NP, 6, :], small[0:NP, 5, :], ACT.Sqrt).then_inc(s["root_ready"], 1)
            a.activation(small[0:NP, 7, :], small[0:NP, 2, :], ACT.Sqrt).then_inc(s["root_ready"], 1)
            act.wait_ge(s["log_arg"], 1)
            a.activation(small[0:NP, 9, :], small[0:NP, 8, :], ACT.Ln).then_inc(s["log_ready"], 1)
            act.wait_ge(s["coef_ready"], 1)
            act.wait_ge(s["table_tails"], 1)
            for b in range(NB):
                act.wait_ge(s["ht_ps"], b + 1)
                wait(act, "pq_ps", b - 1)
                a.activation(hT[:, b % 2, 0:2 * NP], turn_ps[b % 2][:, 0:2 * NP], ACT.Copy).then_inc(s["ht_sb"], 1)
                act.wait_ge(s["pq_ps"], b + 1)
                wait(act, "rest_ready", 2 * (b - 1))
                a.activation(pf[0:NP, b % 2, :], z_ps[b % 2][0:NP, 0:D], ACT.Copy,
                             scale=small[0:NP, 11, b:b + 1]).then_inc(s["pf_ready"], 1)
                a.activation(parts[0][0:NP, b, 0:D], h[:, b, :], ACT.Copy).then_inc(s["part0"], 1)
                act.wait_ge(s["pf_ready"], b + 1)
                a.activation(parts[0][0:NP, b, D:2 * D], pf[0:NP, b % 2, :], ACT.Copy).then_inc(s["part0"], 1)
                act.wait_ge(s["rest_ready"], 2 * b + 2)
                a.activation(parts[1][0:NP, b, :].rearrange("p (a d) -> p a d", a=2), rest[0:NP, :, :], ACT.Copy) \
                    .then_inc(s["part1"], 1)

            def copy_turned(gr, j):
                slot = j % 2
                wait(act, "at_ready", at(gr, PG, j + 1))
                wait(act, "expanded", at(gr, PG, j - 1))
                a.activation(onehot_t[:, slot, :, :].rearrange("p k e -> p (k e)"), at_ps[slot], ACT.Copy) \
                    .then_inc(s["at_copied"], 1)

            def hidden_layer(gr, j):
                slot = j % 2
                wait(act, "expanded", at(gr, PG, j + 1))
                wait(act, "dot_done", at(gr, TG, 2 * j - 2))
                a.activation(hidden[:, slot, :, :], two(z_ps[slot]), ACT.Silu) \
                    .then_inc(s["silu_done"], 1)

            def square_tangents(gr, j):
                par = gr[1] % 2
                for k in range(2):
                    wait(act, "u_ready", at(gr, TG, 2 * j + k + 1))
                    wait(act, "sq_done", at(gr, TG, 2 * j + k - 1))
                    a.activation(square_out[:, k, 0:D - 1], tangents[:, par, 2 * j + k, 1:D], ACT.Square,
                                 accum_out=uu[:, par, 2 * j + k:2 * j + k + 1]).then_inc(s["sq_done"], 1)

            def weights(gr):
                par = gr[1] % 2
                asks = (
                    (2, wt[2], wt[1], ACT.Ln, -1.0, 0.0),
                    (2, wt[3], wt[2], ACT.Exp, 0.5, 0.0),
                    (2, wt[4], logit[:, par, :], ACT.Exp, -1.0, nb2col[:, :]),
                    (3, wt[6], wt[5], ACT.Ln, 1.0, 0.0),
                    (12, wt[2], wt[0], ACT.Ln, 1.0, 0.0),
                    (12, wt[3], wt[2], ACT.Exp, 0.5, 0.0))
                wait(act, "dot_done", at(gr, TG, TG))
                for n, (after, o, i, f, scale, bias) in enumerate(asks):
                    wait(act, "w_vec", at(gr, CHAIN, after))
                    wait(act, "w_act", at(gr, CHAIN_A, n))
                    a.activation(o[:, :], i if n == 2 else i[:, :], f, scale=scale, bias=bias).then_inc(s["w_act"], 1)

            def act_group(gr):
                for j in range(PG):
                    copy_turned(gr if j + 1 < PG else back(gr, -1), (j + 1) % PG)
                    hidden_layer(gr, j)
                    if j:
                        square_tangents(gr, j - 1)
                square_tangents(gr, PG - 1)
                weights(gr)

            def act_first(gr):
                copy_turned(gr, 0)
                act_group(gr)

            groups(act, act_first, act_group, lambda gr: None)

            for b in range(NB):
                act.wait_ge(s["self_u"], b + 1)
                act.wait_ge(s["self_sq"], b) if b else act.wait_ge(s["sq_done"], J)
                a.activation(square_out[0:NP, 0, 0:D - 1], dot_out[0:NP, b % 2, 1:D], ACT.Square,
                             accum_out=small[0:NP, 17, b:b + 1]).then_inc(s["self_sq"], 1)
            n_said = [0]

            def say(o, i, f, scale=1.0):
                n_said[0] += 1
                act.wait_ge(s["tail_ask"], n_said[0])
                a.activation(small[0:NP, o, :], small[0:NP, i, :], f, scale=scale).then_inc(s["tail_say"], 1)

            say(20, 19, ACT.Sqrt, -1.0)
            say(22, 21, ACT.Ln)
            say(20, 19, ACT.Sqrt)
            for q in range(NQ):
                n_cols = len(quad(q)) * NP
                act.wait_ge(s["t_ps"], q + 1)
                wait(act, "m1_ps", 2 * (q - 1))
                for c in range(2):
                    a.activation(sumT[q % 2][:, c, 0:n_cols], turn_ps[c][:, 0:n_cols], ACT.Copy, scale=0.01) \
                        .then_inc(s["t_sb"], 1)
                for f in range(2):
                    act.wait_ge(s["m1_ps"], 2 * q + f + 1)
                    wait(act, "m2_ps", 4 * (q - 1))
                    a.activation(hidT[q % 2][:, f, 0:n_cols], z_ps[f][:, 0:n_cols], ACT.Silu,
                                 bias=mb1col[:, f:f + 1]).then_inc(s["m1_sb"], 1)
            for b in range(NB):
                act.wait_ge(s["o_ready"], b + 1)
                act.wait_ge(s["o_sq"], b) if b else None
                a.activation(square_out[0:NP, 1, 0:D - 1], sums[0:NP, b, 1:D], ACT.Square,
                             accum_out=small[0:NP, 18, b:b + 1]).then_inc(s["o_sq"], 1)
            say(4, 3, ACT.Sqrt)
            say(5, 4, ACT.Exp)
            say(6, 4, ACT.Exp, -1.0)
            for b in range(NB):
                act.wait_ge(s["y_ready"], b + 1)
                act.wait_ge(s["y_sq"], b) if b else None
                a.activation(square_out[0:NP, 1, 0:D - 1], sums[0:NP, b, 1:D], ACT.Square,
                             accum_out=small[0:NP, 13, b:b + 1]).then_inc(s["y_sq"], 1)
            say(15, 14, ACT.Sqrt)

        @block.vector
        def _(dve):
            v = nc.vector
            n = [0]

            def step(ins):
                n[0] += 1
                ins.then_inc(s["vec"], 1)
                dve.wait_ge(s["vec"], n[0])

            def sm(k, rows=NP):
                return small[0:rows, k, :]

            dve.wait_ge(s["edges_in"], 48)
            step(v.tensor_copy(src_f, src_i))
            step(v.tensor_scalar(buck, src_f, 1.0 / NP, 0.5 / NP - 0.5, ALU.mult, ALU.add))
            step(v.tensor_scalar(buck, buck, MAGIC, None, ALU.add))
            step(v.tensor_scalar(buck, buck, -MAGIC, None, ALU.add))
            step(v.scalar_tensor_tensor(local, buck, -float(NP), src_f, ALU.mult, ALU.add))
            for b in range(NB):
                step(v.tensor_scalar(ind, buck, float(b), None, ALU.is_equal, ALU.add,
                                     accum_out=counts[0:NP, b:b + 1]))
            dve.nop().then_inc(s["counted"], 1)
            step(v.memset(ones_row, 1.0))
            step(v.memset(rec_src[:, :, 3], 0.0))
            step(v.tensor_copy(rec_src[:, :, 0], local))
            step(v.tensor_copy(rec_src.bitcast(i32)[:, :, 1], dst_i))
            step(v.tensor_copy(rec_src[:, :, 2], dist_in))
            dve.wait_ge(s["consts_ready"], 1)
            dve.wait_ge(s["count_ps"], 1)
            step(v.tensor_scalar(off[:, 0, :], agg_ps[1][:, 0:NB], 1.0 / PAIR, (PAIR - 1.0) / PAIR - 0.498,
                                 ALU.mult, ALU.add))
            step(v.tensor_scalar(off[:, 0, :], off[:, 0, :], MAGIC, None, ALU.add))
            step(v.tensor_scalar(off[:, 0, :], off[:, 0, :], -MAGIC, None, ALU.add))
            step(v.tensor_tensor_scan(off[:, 1, :], ones[:, 0:NB], off[:, 0, :], 0.0, ALU.mult, ALU.add))
            step(v.tensor_tensor(off[:, 2, :], off[:, 1, :], off[:, 0, :], ALU.subtract))
            step(v.scalar_tensor_tensor(off[0:NP, 3, :], off[0:NP, 2, :], float(PAIR), agg_ps[0][0:NP, 0:NB],
                                        ALU.mult, ALU.add))
            step(v.tensor_scalar(off[0:NP, 4, :], off[0:NP, 3, :], -1.0, None, ALU.add))
            dve.nop().then_inc(s["base_done"], 1)
            for b in range(NB):
                step(v.tensor_scalar(ind, buck, float(b), None, ALU.is_equal))
                step(v.tensor_tensor_scan(scan, ones_row, ind, off[0:NP, 4, b:b + 1], ALU.mult, ALU.add))
                if b == 0:
                    step(v.tensor_tensor(pos, ind, scan, ALU.mult))
                else:
                    step(v.tensor_tensor(tmp, ind, scan, ALU.mult))
                    step(v.tensor_tensor(pos, pos, tmp, ALU.add))
            step(v.tensor_copy(pos_i, pos))
            step(v.tensor_scalar(lo_i, pos_i, P - 1, None, ALU.bitwise_and))
            step(v.tensor_scalar(hi_i, pos_i, P.bit_length() - 1, None, ALU.logical_shift_right))
            step(v.tensor_copy(src_f, lo_i))
            step(v.tensor_copy(tmp, hi_i))
            step(v.scalar_tensor_tensor(pos, src_f, float(J), tmp, ALU.mult, ALU.add))
            step(v.tensor_copy(row_i, pos))
            dve.nop().then_inc(s["sort_done"], 1)
            step(v.memset(pair_acc[:, :], 0.0))
            for b in range(NB - 1):
                step(v.scalar_tensor_tensor(pair_acc[:, :], pair_iota[:, :], off[0:1, 1, b:b + 1], pair_acc[:, :],
                                            ALU.is_ge, ALU.add))
            step(v.tensor_copy(bucket_of[:, :], pair_acc[:, :]))
            dve.nop().then_inc(s["buckets_ready"], 1)

            dve.wait_ge(s["weights_in"], 16 * 9)
            step(v.tensor_scalar(nb2col[:, :], b2col[:, :], -1.0, None, ALU.mult))
            step(v.tensor_copy(w1c_parts[:, 0, :], w1c[:, :]))
            step(v.tensor_tensor(w1c[:, :], w1c[:, :], w1c_parts[:, 0, :], ALU.subtract))
            step(v.tensor_copy(w1c_parts[:, 1, :], w1c[:, :]))
            step(v.tensor_tensor(w1c_parts[:, 2, :], w1c[:, :], w1c_parts[:, 1, :], ALU.subtract))
            dve.nop().then_inc(s["w1c_split"], 1)

            dve.wait_ge(s["x_in"], 16)
            for b in range(NB):
                step(v.bn_stats(stats[0:NP, b % 2, :], xin[:, b, :]))
                step(v.bn_aggr(meanvar[0:NP, b, :], stats[0:NP, b % 2, :]))
            step(v.tensor_scalar(sm(0), meanvar[0:NP, :, 1], 1e-5, None, ALU.add))
            dve.nop().then_inc(s["var_ready"], 1)
            dve.wait_ge(s["std_ready"], 1)
            step(v.reciprocal(sm(3), sm(1)))
            for b in range(NB):
                step(v.tensor_scalar(h[:, b, :], xin[:, b, :], meanvar[0:NP, b, 0:1], small[0:NP, 3, b:b + 1],
                                     ALU.subtract, ALU.mult))
            step(v.tensor_scalar(h, h, 0.0, None, ALU.max))
            dve.nop().then_inc(s["h_ready"], 1)
            step(v.tensor_scalar(sm(3), h[:, :, 0], 1.0 + EPS, None, ALU.max))
            step(v.tensor_scalar(sm(4), sm(3), -1.0, None, ALU.add))
            step(v.scalar_tensor_tensor(sm(5), sm(3), 1.0, sm(4), ALU.add, ALU.mult))
            dve.nop().then_inc(s["theta_ready"], 1)
            dve.wait_ge(s["root_ready"], 2)
            step(v.tensor_tensor(sm(8), sm(6), sm(3), ALU.add))
            dve.nop().then_inc(s["log_arg"], 1)
            step(v.tensor_scalar(sm(7), sm(7), 1e-15, None, ALU.max))
            step(v.reciprocal(sm(10), sm(7)))
            dve.wait_ge(s["log_ready"], 1)
            step(v.tensor_tensor(sm(11), sm(9), sm(10), ALU.mult))
            dve.nop().then_inc(s["coef_ready"], 1)
            step(v.tensor_tensor(sm(12), h[:, :, 0], h[:, :, 0], ALU.mult))
            step(v.tensor_tensor(sm(12), sm(2), sm(12), ALU.subtract))
            step(v.tensor_scalar(sm(12), sm(12), SELF_MAX, None, ALU.min))
            dve.wait_ge(s["table_tails"], 1)
            for b in range(NB):
                dve.wait_ge(s["pq_ps"], b + 1)
                v.scalar_tensor_tensor(xin[:, b, :], h_ps[b % 2][0:NP, 0:D], small[0:NP, 11, b:b + 1],
                                       b1row[0:NP, :], ALU.mult, ALU.add).then_inc(s["q_ready"], 1)
                dve.wait_ge(s["part0"], 2 * b + 2)
                v.tensor_tensor(rest[0:NP, 0, :], h[:, b, :], parts[0][0:NP, b, 0:D], ALU.subtract) \
                    .then_inc(s["rest_ready"], 1)
                v.tensor_tensor(rest[0:NP, 1, :], pf[0:NP, b % 2, :], parts[0][0:NP, b, D:2 * D], ALU.subtract) \
                    .then_inc(s["rest_ready"], 1)
                dve.wait_ge(s["part1"], b + 1)
                v.tensor_tensor(parts[2][0:NP, b, :].rearrange("p (a d) -> p a d", a=2), rest[0:NP, :, :],
                                parts[1][0:NP, b, :].rearrange("p (a d) -> p a d", a=2),
                                ALU.subtract).then_inc(s["part2"], 1)
                dve.wait_ge(s["part2"], b + 1)
            dve.wait_ge(s["slot_filled"], 2 * (EC // SC))
            step(v.memset(sums[:, :, :], 0.0))
            dve.wait_ge(s["recs_in"], 16)
            dve.wait_ge(s["defaults"], 1)
            step(v.tensor_copy(dist_parts[:, :, 0], recs[:, :, 2]))
            step(v.tensor_tensor(rest_d, recs[:, :, 2], dist_parts[:, :, 0], ALU.subtract))
            step(v.tensor_copy(dist_parts[:, :, 1], rest_d))
            step(v.tensor_tensor(dist_parts[:, :, 2], rest_d, dist_parts[:, :, 1], ALU.subtract))

            dve.nop().then_inc(s["agg_added"], 1)
            dve.nop().then_inc(s["agg_added"], 1)
            bucket = [v.alloc_register(f"dve_bucket{j}") for j in range(PG)]

            def build_onehots(gr, j):
                wait(dve, "at_ready", at(gr, PG, j + 1 - PG))
                for k in range(2):
                    v.tensor_scalar(onehot[:, 2 * j + k, 0:NP], iota_b[:, 0:NP],
                                    recs[:, bass.ds(at(gr, TG, 2 * j + k), 1), 0], None,
                                    ALU.is_equal).then_inc(s["onehots"], 1)
                v.tensor_copy(onehot[:, 2 * j:2 * j + 2, NP:P], dist_parts[:, bass.ds(at(gr, TG, 2 * j), 2), :]) \
                    .then_inc(s["onehots"], 1)

            def tangent(gr, j):
                slot, half, par = j % 2, j // (PG // 2), gr[1] % 2
                c = (2 * j) % HT
                wait(dve, "expanded", at(gr, PG, j + 1))
                v.scalar_tensor_tensor(neg0[:, slot, :], two(h_ps[slot])[:, :, 0], -1.0,
                                       gathered[:, half, c:c + 2, 0], ALU.mult, ALU.mult).then_inc(s["neg_done"], 1)
                wait(dve, "neg_done", at(gr, PG, j + 1))
                for k in range(2):
                    v.tensor_tensor_reduce(out=mink_out[:, k, 0:D - 1], in0=h_ps[slot][:, k * D + 1:(k + 1) * D],
                                           in1=gathered[:, half, c + k, 1:D], scale=1.0,
                                           scalar=neg0[:, slot, k:k + 1], op0=ALU.mult, op1=ALU.add,
                                           accum_out=mink[:, 2 * j + k:2 * j + k + 1]).then_inc(s["mink_done"], 1)
                wait(dve, "mink_done", at(gr, TG, 2 * j + 2))
                v.tensor_scalar(xy[:, par, 2 * j:2 * j + 2], mink[:, 2 * j:2 * j + 2], SELF_MAX, None,
                                ALU.min).then_inc(s["xy_done"], 1)
                wait(dve, "xy_done", at(gr, PG, j + 1))
                for k in range(2):
                    v.scalar_tensor_tensor(tangents[:, par, 2 * j + k, :], h_ps[slot][:, k * D:(k + 1) * D],
                                           xy[:, par, 2 * j + k:2 * j + k + 1], gathered[:, half, c + k, 0:D],
                                           ALU.mult, ALU.add).then_inc(s["u_ready"], 1)

            def attention_dot(gr, j):
                slot, par = j % 2, gr[1] % 2
                wait(dve, "silu_done", at(gr, PG, j + 1))
                wait(dve, "dot_done", at(gr, TG, 2 * j))
                for k in range(2):
                    v.tensor_tensor_reduce(out=dot_out[:, k, :], in0=hidden[:, slot, k, :], in1=w2row[:, :],
                                           scale=1.0, scalar=0.0, op0=ALU.mult, op1=ALU.add,
                                           accum_out=logit[:, par, 2 * j + k:2 * j + k + 1]) \
                        .then_inc(s["dot_done"], 1)

            def weigh_onehots(gr, j):
                slot, par = j % 2, gr[1] % 2
                if j >= 2:
                    wait(dve, "agg_summed", at(gr, PG, j - 1))
                for k in range(2):
                    v.tensor_scalar(weighted[:, slot, k, 0:NP], iota_f[:, 0:NP],
                                    recs[:, bass.ds(at(gr, TG, 2 * j + k), 1), 0],
                                    weight[:, par, 2 * j + k:2 * j + k + 1],
                                    ALU.is_equal, ALU.mult).then_inc(s["weighted_ready"], 1)

            def add_sums(gr, j):
                wait(dve, "agg_summed", at(gr, PG, j + 1))
                wait(dve, "agg_added", at(gr, PG, j + 2))
                b = v.snap(bucket[j])
                v.tensor_tensor(sums[0:NP, bass.ds(b, 1), :], agg_ps[j % 2][0:NP, None, 0:D],
                                sums[0:NP, bass.ds(b, 1), :], ALU.add).then_inc(s["agg_added"], 1)

            def load_buckets(gr):
                for j in range(PG):
                    v.reg_load(bucket[j], bucket_of[0:1, bass.ds(at(gr, PG, j), 1)])

            def vec_group(gr, sum_last=True):
                par = gr[1] % 2
                last = back(gr)
                xys = xy[:, par, :]
                done = [0]

                def chain(ins):
                    done[0] += 1
                    ins.then_inc(s["w_vec"], 1)
                    wait(dve, "w_vec", at(gr, CHAIN, done[0]))

                if sum_last:
                    load_buckets(last)
                for j in range(PG):
                    build_onehots(gr if j + 2 < PG else back(gr, -1), (j + 2) % PG)
                    tangent(gr, j)
                    if j:
                        attention_dot(gr, j - 1)
                    if sum_last and j < LATE:
                        weigh_onehots(last, j)
                        if j:
                            add_sums(last, j - 1)
                attention_dot(gr, PG - 1)
                chain(v.tensor_scalar(wt[0][:, :], xys, -1.0, -1.0, ALU.mult, ALU.add))
                chain(v.scalar_tensor_tensor(wt[1][:, :], xys, 1.0, wt[0][:, :], ALU.subtract, ALU.mult))
                if sum_last:
                    weigh_onehots(last, LATE)
                    add_sums(last, LATE - 1)
                wait(dve, "w_act", at(gr, CHAIN_A, 2))
                chain(v.tensor_tensor(wt[5][:, :], wt[3][:, :], xys, ALU.subtract))
                chain(v.tensor_tensor(wt[7][:, :], tangents[:, par, :, 0], tangents[:, par, :, 0], ALU.mult))
                wait(dve, "sq_done", at(gr, TG, TG))
                chain(v.tensor_tensor(wt[8][:, :], uu[:, par, :], wt[7][:, :], ALU.subtract))
                chain(v.tensor_scalar(wt[8][:, :], wt[8][:, :], EPS, None, ALU.max))
                chain(v.reciprocal(wt[9][:, :], wt[8][:, :]))
                wait(dve, "w_act", at(gr, CHAIN_A, 3))
                chain(v.tensor_scalar(wt[10][:, :], wt[4][:, :], 1.0, None, ALU.add))
                chain(v.reciprocal(wt[11][:, :], wt[10][:, :]))
                chain(v.tensor_tensor(wt[12][:, :], wt[11][:, :], recs[:, bass.ds(at(gr, TG, 0), TG), 2], ALU.mult))
                wait(dve, "w_act", at(gr, CHAIN_A, 4))
                chain(v.tensor_tensor(wt[13][:, :], wt[6][:, :], wt[6][:, :], ALU.mult))
                chain(v.scalar_tensor_tensor(wt[0][:, :], wt[13][:, :], 50.0, wt[9][:, :], ALU.min, ALU.mult))
                if sum_last:
                    for j in range(LATE + 1, PG):
                        weigh_onehots(last, j)
                        add_sums(last, j - 1)
                    add_sums(last, PG - 1)
                wait(dve, "w_act", at(gr, CHAIN_A, 6))
                chain(v.tensor_tensor(weight[:, par, :], wt[12][:, :], wt[3][:, :], ALU.mult))

            def vec_first(gr):
                build_onehots(gr, 0)
                build_onehots(gr, 1)
                vec_group(gr, sum_last=False)

            def vec_last(gr):
                load_buckets(gr)
                for j in range(PG):
                    weigh_onehots(gr, j)
                    if j:
                        add_sums(gr, j - 1)
                add_sums(gr, PG - 1)

            groups(dve, vec_first, vec_group, vec_last)

            dve.wait_ge(s["h_back"], 16)
            dve.wait_ge(s["agg_added"], NPAIR + 2)
            step(v.tensor_scalar(sm(14), h[:, :, 0], EPS, None, ALU.max))
            step(v.reciprocal(sm(0), sm(14)))
            for b in range(NB):
                step(v.tensor_tensor_reduce(out=mink_out[0:NP, 0, 0:D - 1], in0=h[:, b, 1:D], in1=sums[0:NP, b, 1:D],
                                            scale=1.0, scalar=0.0, op0=ALU.mult, op1=ALU.add,
                                            accum_out=small[0:NP, 16, b:b + 1]))
            step(v.tensor_tensor(sums[0:NP, :, 0], sm(16), sm(0), ALU.mult))
            dve.nop().then_inc(s["tail_agg"], 1)
            for b in range(NB):
                wait(dve, "self_sq", b - 1)
                v.scalar_tensor_tensor(dot_out[0:NP, b % 2, :], h[:, b, :], small[0:NP, 12, b:b + 1], h[:, b, :],
                                       ALU.mult, ALU.add).then_inc(s["self_u"], 1)
            dve.wait_ge(s["self_sq"], NB)

            asked = [0]

            def ask():
                asked[0] += 1
                dve.nop().then_inc(s["tail_ask"], 1)
                dve.wait_ge(s["tail_say"], asked[0])

            step(v.tensor_tensor(sm(1), h[:, :, 0], sm(12), ALU.mult))
            step(v.tensor_tensor(sm(1), sm(1), h[:, :, 0], ALU.add))
            step(v.tensor_tensor(sm(1), sm(1), sm(1), ALU.mult))
            step(v.tensor_tensor(sm(2), sm(17), sm(1), ALU.subtract))
            step(v.tensor_scalar(sm(2), sm(2), EPS, None, ALU.max))
            step(v.reciprocal(sm(3), sm(2)))
            step(v.tensor_scalar(sm(4), sm(12), -1.0, -1.0, ALU.mult, ALU.add))
            step(v.scalar_tensor_tensor(sm(19), sm(12), 1.0, sm(4), ALU.subtract, ALU.mult))
            ask()
            step(v.tensor_tensor(sm(21), sm(20), sm(12), ALU.subtract))
            ask()
            step(v.tensor_tensor(sm(5), sm(22), sm(22), ALU.mult))
            step(v.scalar_tensor_tensor(sm(19), sm(5), 50.0, sm(3), ALU.min, ALU.mult))
            ask()
            for b in range(NB):
                dve.wait_ge(s["m2_ps"], b + 1)
                step(v.tensor_tensor(sums[0:NP, b, :], agg_ps[b % 2][0:NP, 0:D], mb2row[0:NP, :], ALU.add))
                dve.nop().then_inc(s["m2_sb"], 1)
                step(v.scalar_tensor_tensor(mink_out[0:NP, 1, :], h[:, b, :], small[0:NP, 12, b:b + 1], h[:, b, :],
                                            ALU.mult, ALU.add))
                step(v.scalar_tensor_tensor(sums[0:NP, b, :], mink_out[0:NP, 1, :], small[0:NP, 20, b:b + 1],
                                            sums[0:NP, b, :], ALU.mult, ALU.add))
                dve.nop().then_inc(s["o_ready"], 1)
                step(v.tensor_tensor_reduce(out=mink_out[0:NP, 0, 0:D - 1], in0=h[:, b, 1:D], in1=sums[0:NP, b, 1:D],
                                            scale=1.0, scalar=0.0, op0=ALU.mult, op1=ALU.add,
                                            accum_out=small[0:NP, 16, b:b + 1]))
            dve.wait_ge(s["o_sq"], NB)
            step(v.tensor_tensor(sm(1), sm(16), sm(0), ALU.mult))
            step(v.tensor_tensor(sm(2), sm(1), sm(1), ALU.mult))
            step(v.tensor_tensor(sm(3), sm(18), sm(2), ALU.subtract))
            step(v.tensor_scalar(sm(3), sm(3), EPS, None, ALU.max))
            ask()
            step(v.tensor_scalar(sm(4), sm(4), 1e6, 1e-15, ALU.min, ALU.max))
            ask()
            ask()
            step(v.tensor_tensor(sm(7), sm(5), sm(6), ALU.add))
            step(v.tensor_scalar(sm(7), sm(7), 0.5, None, ALU.mult))
            step(v.tensor_tensor(sm(8), sm(5), sm(6), ALU.subtract))
            step(v.reciprocal(sm(9), sm(4)))
            step(v.scalar_tensor_tensor(sm(8), sm(8), 0.5, sm(9), ALU.mult, ALU.mult))
            step(v.tensor_tensor(sm(9), sm(4), sm(4), ALU.mult))
            step(v.tensor_scalar(sm(9), sm(9), 1.0, None, ALU.min))
            step(v.tensor_scalar(sm(10), sm(4), 1.0, None, ALU.is_lt))
            step(v.tensor_scalar(sm(11), sm(4), 1.0, None, ALU.is_ge))
            for o, terms in ((21, (90.0, 56.0, 30.0, 12.0, 2.0)), (22, (110.0, 72.0, 42.0, 20.0, 6.0))):
                step(v.tensor_scalar(sm(o), sm(9), 1.0 / terms[0], 1.0, ALU.mult, ALU.add))
                for term in terms[1:]:
                    step(v.tensor_tensor(sm(o), sm(o), sm(9), ALU.mult))
                    step(v.tensor_scalar(sm(o), sm(o), 1.0 / term, 1.0, ALU.mult, ALU.add))
            for e, o in ((7, 21), (8, 22)):
                step(v.tensor_tensor(sm(e), sm(e), sm(11), ALU.mult))
                step(v.tensor_tensor(sm(o), sm(o), sm(10), ALU.mult))
                step(v.tensor_tensor(sm(e), sm(e), sm(o), ALU.add))
            for b in range(NB):
                step(v.tensor_scalar(sums[0:NP, b, :], sums[0:NP, b, :], small[0:NP, 8, b:b + 1], None, ALU.mult))
                step(v.scalar_tensor_tensor(sums[0:NP, b, :], h[:, b, :], small[0:NP, 7, b:b + 1], sums[0:NP, b, :],
                                            ALU.mult, ALU.add))
                dve.nop().then_inc(s["y_ready"], 1)
            dve.wait_ge(s["y_sq"], NB)
            step(v.tensor_scalar(sm(14), sm(13), 1.0, None, ALU.add))
            ask()
            step(v.tensor_copy(sums[0:NP, :, 0], sm(15)))
            dve.wait_ge(s["x_back"], 16)
            step(v.tensor_tensor(xin, xin, sums[0:NP, :, :], ALU.add))
            dve.nop().then_inc(s["out_ready"], 1)


_INS = ["x", "src", "dst", "edge_weight1", "L0_gnn_att_w1", "L0_gnn_att_b1", "L0_gnn_att_w2", "L0_gnn_att_b2",
        "L0_gnn_mlp_w1", "L0_gnn_mlp_b1", "L0_gnn_mlp_w2", "L0_gnn_mlp_b2"]


def kernel(**inputs):
    import numpy as _np
    import concourse.bacc as _bacc
    from concourse import mybir as _mybir
    from concourse.bass_utils import run_bass_kernel_spmd as _run

    nc = _bacc.Bacc("TRN2", target_bir_lowering=False, num_devices=1)
    arrays, args = {}, []
    for name in _INS:
        a = _np.ascontiguousarray(inputs[name])
        if name == "edge_weight1":
            a = a.reshape(-1)
        arrays[f"in_{name}_dram"] = a
        args.append(nc.dram_tensor(f"in_{name}_dram", a.shape, _mybir.dt.from_np(a.dtype), kind="ExternalInput").ap())
    shape = inputs["x"].shape
    args.append(nc.dram_tensor("out_0_dram", shape, _mybir.dt.from_np(_np.dtype("float32")),
                               kind="ExternalOutput").ap())
    hyperbolic_gnn_layer(nc, *args)
    r = _run(nc, [arrays], core_ids=[0])
    return r.results[0]["out_0_dram"]
```

```python
import concourse.bass as bass
from concourse import mybir
from contextlib import ExitStack


def hyperbolic_gnn_layer(nc, x, src, dst, dist, att_w1, att_b1, att_w2, att_b2,
                         mlp_w1, mlp_b1, mlp_w2, mlp_b2, out):
    fp32 = mybir.dt.float32
    bf16 = mybir.dt.bfloat16
    i32 = mybir.dt.int32
    ALU = mybir.AluOpType
    ACT = mybir.ActivationFunctionType
    AX = mybir.AxisListType

    N, D = x.shape
    E = src.shape[0]
    P = 128
    NP = 125
    NB = N // NP
    EC = E // NP
    PAIR = 2 * P
    TG = 16
    PG = TG // 2
    LAG = 12
    NPAIR = (E + NB * (PAIR - 1)) // PAIR
    NG = -(-NPAIR // PG)
    assert NB * NP == N and EC * NP == E and NG % 2 == 1
    NPAIR = NG * PG
    J = 2 * NPAIR
    EPS = 1e-7
    SELF_MAX = -1.0000001
    MAGIC = 12582912.0
    NQ = -(-NB // 4)
    CHAIN = 11
    CHAIN_A = 6
    SC = 19
    MOVED = 140
    HOT = 4
    assert MOVED % HOT == 0 and (EC - MOVED) % SC == 0
    SCATTERS = (EC - MOVED) // SC
    LOW = 64
    WORD = 4096
    assert N < WORD
    ROOT50 = 50.0 ** 0.5

    sorted_dram = nc.dram_tensor("sorted_edges", (P * J, 2), fp32).ap()
    node_dram = nc.dram_tensor("node_rows", (N, 2 * D), fp32).ap()

    ctx = ExitStack()
    with ctx:
        def sb(name, shape, dt=fp32):
            return ctx.enter_context(nc.sbuf_tensor(name, shape, dt))

        def pb(name, shape, dt=fp32):
            return ctx.enter_context(nc.psum_tensor(name, shape, dt))

        def sem(name):
            return ctx.enter_context(nc.semaphore(name))

        parts = [sb(f"node_part{k}", [P, NB, 2 * D], bf16) for k in range(3)]
        sums = sb("sums", [P, NB, D])
        gathered = sb("gathered", [P, PG, 2, 2 * D])
        tangents = sb("tangents", [P, 2, TG, D])
        recs = sb("recs", [P, J + 6, 4])
        dist_parts = sb("dist_parts", [P, J + 6, 3], bf16)
        onehot = sb("onehot", [P, 2 * TG, P], bf16)
        onehot_t = sb("onehot_t", [P, 2, 2, P], bf16)
        weighted = sb("weighted", [P, 2, 2, P])
        hidden = sb("hidden", [P, 2, 2, D])
        dot_out = sb("dot_out", [P, 2, D], bf16)
        mink_out = sb("mink_out", [P, 2, D], bf16)
        square_out = sb("square_out", [P, 2, D], bf16)
        ident = sb("ident", [P, P])
        ident_b = sb("ident_b", [P, P], bf16)
        iota_f = sb("iota_f", [P, P])
        iota_b = sb("iota_b", [P, P], bf16)
        ones = sb("ones", [P, P])
        before = sb("before", [P, P])
        w2row = sb("w2row", [P, D])
        mb2row = sb("mb2row", [P, D])
        mb1col = sb("mb1col", [P, 2])
        b2col = sb("b2col", [P, 1])
        nb2col = sb("nb2col", [P, 1])
        idx_now = sb("idx_now", [P, PG, 2], i32)
        bucket_of = sb("bucket_of", [1, NPAIR + 1], i32)
        neg0 = sb("neg0", [P, 2, 2])
        mink = sb("mink", [P, TG])
        xy = sb("xy", [P, 2, TG])
        uu = sb("uu", [P, 2, TG])
        logit = sb("logit", [P, 2, TG])
        wt = [sb(f"wt{k}", [P, TG]) for k in range(13)]
        weight = sb("weight", [P, 2, TG])
        small = sb("small", [P, 24, NB])
        counts = sb("counts", [P, NB])
        off = sb("off", [P, 5, NB])
        stats = sb("stats", [P, 2, 6])
        meanvar = sb("meanvar", [P, NB, 2])

        sort = sums[:, :, :].rearrange("p b d -> p (b d)")

        def col(k):
            return sort[0:NP, k * EC:(k + 1) * EC]

        src_i = col(0).bitcast(i32)
        dst_i = col(1).bitcast(i32)
        dist_in = col(2)
        src_f, buck, local, pos, ind, scan, tmp = (col(k) for k in range(3, 10))
        pos_i, lo_i, hi_i, row_i = (col(k).bitcast(i32) for k in (0, 7, 8, 0))
        ones_row = col(14)
        rec_src = sort[0:NP, 10 * EC:12 * EC].rearrange("p (t c) -> p t c", c=2)
        slot_f, tile_f = src_f, tmp
        word_parts = (col(12), col(14), col(13))
        dst_f = col(13)
        dist_terms = (col(4), col(5), col(6))
        rough = col(7).bitcast(bf16)[:, 0:EC]
        flat_recs = recs[:, :, :].rearrange("p j c -> p (j c)")
        tile_iota = flat_recs[:, 0:J]
        tile_hot = flat_recs[:, J:J + HOT * J // 2].bitcast(bf16).rearrange("p (a j) -> p a j", a=HOT)
        slot_hot = onehot[:, 0:HOT, :]
        slot_val = onehot[:, HOT:7 * HOT, :].rearrange("p (a k) m -> p a k m", a=HOT)
        raw = sort[:, 0:2 * J].rearrange("p (j c) -> p j c", c=2)
        word = sort[:, 2 * J:3 * J]
        word_i, high_i = (sort[:, k * J:(k + 1) * J].bitcast(i32) for k in (3, 4))
        xin = tangents[0:NP, :, :, :].rearrange("p a t d -> p (a t) d")[:, 0:NB, :]
        w1 = tangents[:, :, :, :].rearrange("p a t d -> p (a t d)")[:, NB * D:NB * D + 4 * D] \
            .rearrange("p (c d) -> p c d", c=2)
        h = gathered[0:NP, :, :, :].rearrange("p j k d -> p (j k d)")[:, 0:NB * D] \
            .rearrange("p (b d) -> p b d", d=D)
        hT = hidden[:, :, :, :].rearrange("p a i d -> p a (i d)")
        spare = onehot[:, :, :].rearrange("p t n -> p (t n)").bitcast(fp32)
        pf, rest = (spare[:, 2 * k * D:2 * (k + 1) * D].rearrange("p (a d) -> p a d", a=2) for k in range(2))
        w1c = spare[:, 4 * D:5 * D]
        b1row = spare[:, 5 * D:6 * D]
        w1c_parts = onehot[:, :, :].rearrange("p t n -> p (t n)")[:, 12 * D:15 * D].rearrange("p (k d) -> p k d", k=3)
        rest_d = hidden[:, :, :, :].rearrange("p a k d -> p (a k d)")[:, 0:J + 6]
        pair_iota = sb("pair_iota", [1, NPAIR])
        pair_acc = sb("pair_acc", [1, NPAIR])
        slot_idx = sb("slot_idx", [P, 2, SC], i32)
        slot_rec = sb("slot_rec", [P, 2, SC, 2])

        def quad_buffers(k):
            flat = parts[k][:, :, :].rearrange("p b d -> p (b d)").bitcast(fp32)
            return [flat[:, i * 1024:(i + 1) * 1024].rearrange("p (c n) -> p c n", c=2) for i in range(2)]

        sumT, hidT = quad_buffers(0), quad_buffers(1)

        mw1, mw2 = (parts[2][:, 4 * k:4 * k + 2, :].rearrange("p b d -> p (b d)").bitcast(fp32)
                    .rearrange("p (c d) -> p c d", c=2)[:, :, 0:D] for k in range(2))

        def quad(q):
            return range(4 * q, min(NB, 4 * q + 4))

        h_ps, z_ps, turn_ps, agg_ps = ([pb(f"{name}_ps{k}", [P, 2 * D]) for k in range(2)]
                                       for name in ("h", "z", "turn", "agg"))
        at_ps = [t[:, 0:P].bitcast(bf16) for t in turn_ps]

        def two(bank):
            return bank[:, :].rearrange("p (k d) -> p k d", k=2)

        s = {}
        for name in (
                "edges_in", "weights_in", "x_in", "mlp_in",
                "consts_ready", "pool_step", "pool_turn", "defaults", "w1_zeroed", "w1c_split", "tails_zero", "table_tails",
                "fill_out", "vec", "counted", "count_ps", "sort_done", "slot_filled",
                "scattered0", "scattered1", "recs_in", "tile_iota",
                "terms_ready", "hots_built", "hots_scaled", "hots_used", "recs_ready", "base_done",
                "var_ready", "std_ready", "h_ready", "sq_setup", "theta_ready", "root_ready",
                "log_arg", "log_ready", "coef_ready", "ht_ps", "ht_sb", "pq_ps", "pf_ready",
                "part0", "rest_ready", "part1", "part2", "q_ready", "h_out", "q_out",
                "buckets_ready", "idx_ready", *(f"gath{j}" for j in range(PG)), "onehots", "at_ready",
                "at_copied", "expanded", "silu_done", "neg_done", "mink_done", "xy_done",
                "u_ready", "sq_done", "dot_done", "w_vec", "w_act", "weighted_ready",
                "agg_summed", "agg_added", "h_back", "x_back", "tail_agg", "self_u", "self_sq",
                "tail_ask", "tail_say", "t_ps", "t_sb", "m1_ps", "m1_sb", "m2_ps", "m2_sb",
                "o_ready", "o_sq", "y_ready", "y_sq", "out_ready", "out_done"):
            s[name] = sem(name)

        def wait(eng, name, value):
            if not (isinstance(value, int) and value <= 0):
                eng.wait_ge(s[name], value)

        block = ctx.enter_context(nc.Block())

        def groups(eng, body):
            for g in range(3):
                body((0, g))
            with eng.Fori(1, (NG - 1) // 2) as i:
                body((i, 1))
                body((i, 2))

        def at(g, per, plus):
            i, o = g
            return per * o + plus if isinstance(i, int) else i * (2 * per) + (per * o + plus)

        def pair(g, j, n):
            return (g[0], g[1] + (j + n) // PG), (j + n) % PG

        def there(g):
            return not (isinstance(g[0], int) and g[1] < 0)

        def pairs_left(per_pair):
            for n in range(LAG):
                per_pair(*pair((0, NG - 1), PG - LAG, n))

        @block.sync
        def _(sp):
            for a, d in ((src, src_i), (dst, dst_i), (dist, dist_in)):
                sp.dma_start(d, a.rearrange("(p t) -> p t", p=NP)).then_inc(s["edges_in"], 16)
            sp.dma_start(xin, x.rearrange("(b l) d -> l b d", l=NP)).then_inc(s["x_in"], 16)
            for half in range(2):
                sp.dma_start(w1[:, :, half * D:(half + 1) * D],
                             att_w1[half * D:(half + 1) * D, :].rearrange("(c p) d -> p c d", p=P)) \
                    .then_inc(s["weights_in"], 16)
            for a, d in ((att_w1[2 * D:2 * D + 1, :], w1c), (att_b1[None, :], b1row),
                         (att_w2.rearrange("d o -> o d"), w2row), (mlp_b2[None, :], mb2row)):
                sp.dma_start(d[:, :], a.broadcast_to((P, D))).then_inc(s["weights_in"], 16)
            for c in range(2):
                sp.dma_start(mb1col[:, c:c + 1], mlp_b1[c * P:(c + 1) * P][:, None]).then_inc(s["weights_in"], 16)
            sp.dma_start(b2col[:, :], att_b2[None, :].broadcast_to((P, 1))).then_inc(s["weights_in"], 16)
            sp.wait_ge(s["defaults"], 1)
            sp.dma_start(sorted_dram.rearrange("(p j) c -> p (j c)", p=P),
                         flat_recs[:, 0:2 * J]).then_inc(s["fill_out"], 16)
            sp.wait_ge(s["tails_zero"], 1)
            sp.wait_ge(s["w1c_split"], 1)
            for k in range(3):
                sp.dma_start(parts[k][NP:P, :, D:2 * D],
                             w1c_parts[NP:P, k, None, :].broadcast_to((P - NP, NB, D))).then_inc(s["table_tails"], 16)
            rows = node_dram.rearrange("(b l) d -> l b d", l=NP)
            sp.wait_ge(s["h_ready"], 1)
            sp.dma_start(rows[:, :, 0:D], h).then_inc(s["h_out"], 16)
            sp.wait_ge(s["q_ready"], NB)
            sp.dma_start(rows[:, :, D:2 * D], xin).then_inc(s["q_out"], 16)
            sp.wait_ge(s["scattered0"], 16 * SC * ((SCATTERS + 1) // 2))
            sp.wait_ge(s["scattered1"], 16 * SC * (SCATTERS // 2))
            sp.wait_ge(s["hots_built"], 4 * MOVED)
            sp.wait_ge(s["hots_scaled"], 4 * MOVED)
            sp.dma_start(raw.rearrange("p j c -> p (j c)"),
                         sorted_dram.rearrange("(p j) c -> p (j c)", p=P)).then_inc(s["recs_in"], 16)
            sp.wait_ge(s["expanded"], NPAIR)
            sp.wait_ge(s["u_ready"], J)
            sp.dma_start(h, rows[:, :, 0:D]).then_inc(s["h_back"], 16)
            for a, d in ((mlp_w1, mw1), (mlp_w2, mw2)):
                sp.dma_start(d, a.rearrange("(c p) d -> p c d", p=P)).then_inc(s["mlp_in"], 16)
            sp.wait_ge(s["agg_summed"], NPAIR)
            sp.wait_ge(s["sq_done"], J)
            sp.dma_start(xin, x.rearrange("(b l) d -> l b d", l=NP)).then_inc(s["x_back"], 16)
            sp.wait_ge(s["out_ready"], 1)
            sp.dma_start(out.rearrange("(b l) d -> l b d", l=NP), xin).then_inc(s["out_done"], 16)
            sp.wait_ge(s["out_done"], 16)

        @block.gpsimd
        def _(pool):
            n = [0]

            def step(ins):
                n[0] += 1
                ins.then_inc(s["pool_step"], 1)
                pool.wait_ge(s["pool_step"], n[0])

            g = nc.gpsimd
            step(g.memset(recs[:, :, :], 0.0))
            pool.nop().then_inc(s["defaults"], 1)
            step(g.memset(ones[:, :], 1.0))
            step(g.affine_select(out=ident[:, :], in_=ones[:, :], compare_op=ALU.is_equal, fill=0.0, base=0,
                                 pattern=[[-1, P]], channel_multiplier=1))
            step(g.affine_select(out=before[:, :], in_=ones[:, :], compare_op=ALU.is_gt, fill=0.0, base=0,
                                 pattern=[[1, P]], channel_multiplier=-1))
            step(g.tensor_copy(ident_b[:, :], ident[:, :]))
            step(g.iota(pair_iota[:, :], pattern=[[1, NPAIR]], base=0, channel_multiplier=0,
                        allow_small_or_imprecise_dtypes=True))
            step(g.iota(iota_f[:, :], pattern=[[1, P]], base=0, channel_multiplier=0,
                        allow_small_or_imprecise_dtypes=True))
            step(g.tensor_copy(iota_b[:, :], iota_f[:, :]))
            pool.nop().then_inc(s["consts_ready"], 1)
            pool.wait_ge(s["weights_in"], 16 * 9)
            g.memset(w1[0:1, 0, :], 0.0).then_inc(s["w1_zeroed"], 1)
            for k in range(3):
                step(g.memset(parts[k][96:P, :, :], 0.0))
            pool.nop().then_inc(s["tails_zero"], 1)

            pool.wait_ge(s["sort_done"], 1)
            pool.wait_ge(s["fill_out"], 16)
            g.iota(tile_iota, pattern=[[1, J]], base=0, channel_multiplier=0,
                   allow_small_or_imprecise_dtypes=True).then_inc(s["tile_iota"], 1)

            def scatter(i, slot, first_use, count):
                base = i * (2 * SC) + slot * SC
                if not first_use:
                    pool.wait_ge(s[f"scattered{slot}"], count * (16 * SC))
                g.tensor_copy(slot_idx[0:NP, slot, :], row_i[:, bass.ds(base, SC)]).then_inc(s["slot_filled"], 1)
                g.tensor_copy(slot_rec[0:NP, slot, :, :], rec_src[:, bass.ds(base, SC), :]).then_inc(s["slot_filled"], 1)
                pool.wait_ge(s["slot_filled"], i * 4 + 2 * slot + 2)
                pool.nop().then_inc(s["pool_turn"], 1)
                for c in range(SC):
                    g.indirect_dma_start(sorted_dram,
                                         bass.IndirectOffsetOnAxis(ap=slot_idx[0:NP, slot, c:c + 1], axis=0),
                                         slot_rec[0:NP, slot, c, :], None).then_inc(s[f"scattered{slot}"], 16)

            steps = SCATTERS
            scatter(0, 0, True, 0)
            scatter(0, 1, True, 0)
            with pool.Fori(1, steps // 2) as i:
                scatter(i, 0, False, i)
                scatter(i, 1, False, i)
            if steps % 2:
                scatter(steps // 2, 0, False, steps // 2)

            pool.wait_ge(s["recs_ready"], 1)
            pool.wait_ge(s["h_out"], 16)
            pool.wait_ge(s["q_out"], 16)
            pool.wait_ge(s["part2"], NB)
            pool.wait_ge(s["sq_setup"], NB)
            dst_of = recs[:, :, 1].bitcast(i32)

            def gather(gr):
                for j in range(PG):
                    wait(pool, "expanded", at(gr, PG, j + 1 - PG))
                    wait(pool, "u_ready", at(gr, TG, 2 * j + 2 - TG))
                    g.tensor_copy(idx_now[:, j, :], dst_of[:, bass.ds(at(gr, TG, 2 * j), 2)]) \
                        .then_inc(s["idx_ready"], 1)
                    pool.wait_ge(s["idx_ready"], at(gr, PG, j + 1))
                    pool.nop().then_inc(s["pool_turn"], 1)
                    for k in range(2):
                        g.indirect_dma_start(gathered[:, j, k, :], None, node_dram,
                                             bass.IndirectOffsetOnAxis(ap=idx_now[:, j, k:k + 1], axis=0)) \
                            .then_inc(s[f"gath{j}"], 16)

            groups(pool, gather)

        @block.tensor
        def _(pe):
            t = nc.tensor
            pe.wait_ge(s["consts_ready"], 1)
            pe.wait_ge(s["counted"], 1)
            t.matmul(agg_ps[0][0:NP, 0:NB], before[0:NP, 0:NP], counts[0:NP, :], start=True, stop=True)
            t.matmul(agg_ps[1][:, 0:NB], ones[0:NP, :], counts[0:NP, :], start=True, stop=True).then_inc(s["count_ps"], 1)
            pe.wait_ge(s["weights_in"], 16 * 9)
            pe.wait_ge(s["h_ready"], 1)
            pe.wait_ge(s["w1_zeroed"], 1)

            def turn(b):
                wait(pe, "ht_sb", b - 1)
                for c in range(2):
                    last = t.transpose(turn_ps[b % 2][:, c * NP:(c + 1) * NP], h[:, b, c * P:(c + 1) * P],
                                       ident[0:NP, 0:NP])
                last.then_inc(s["ht_ps"], 1)

            def move_column(c, slot, first=False, last=False):
                pe.wait_ge(s["hots_built"], c * 4 + 4)
                pe.wait_ge(s["hots_scaled"], c * 4 + 4)
                for k in range(6):
                    ins = t.matmul(agg_ps[k // 3][:, 0:J], slot_val[0:NP, slot, k, :], tile_hot[0:NP, slot, :],
                                   start=(first and k % 3 == 0), stop=(last and k % 3 == 2))
                ins.then_inc(s["hots_used"], 1)

            turn(0)
            for b in range(NB):
                if b + 1 < NB:
                    turn(b + 1)
                pe.wait_ge(s["ht_sb"], b + 1)
                wait(pe, "pf_ready", b - 1)
                wait(pe, "q_ready", b - 1)
                for bank, half in ((z_ps, 0), (h_ps, 1)):
                    for c in range(2):
                        last = t.matmul(bank[b % 2][0:NP, 0:D], hT[:, b % 2, c * NP:(c + 1) * NP],
                                        w1[:, c, half * D:(half + 1) * D], start=(c == 0), stop=(c == 1))
                last.then_inc(s["pq_ps"], 1)
            for slot in range(HOT):
                move_column(slot, slot, first=(slot == 0))
            with pe.Fori(1, MOVED // HOT - 1) as i:
                for slot in range(HOT):
                    move_column(i * HOT + slot, slot)
            for slot in range(HOT):
                move_column(MOVED - HOT + slot, slot, last=(slot == HOT - 1))

            bucket = [t.alloc_register(f"pe_bucket{j}") for j in range(2)]
            pe.wait_ge(s["buckets_ready"], 1)
            pe.wait_ge(s["part2"], NB)
            pe.wait_ge(s["table_tails"], 48)
            pe.wait_ge(s["sq_setup"], NB)

            def turn_onehots(gr, j):
                slot, ring = j % 2, (gr[1] % 2) * TG + 2 * j
                wait(pe, "onehots", at(gr, 3 * PG, 3 * j + 3))
                wait(pe, "at_copied", at(gr, PG, j - 1))
                for k in range(2):
                    last = t.transpose(at_ps[slot][:, k * P:(k + 1) * P], onehot[:, ring + k, :], ident_b[:, :])
                last.then_inc(s["at_ready"], 1)

            def load_bucket(gr, j):
                t.reg_load(bucket[j % 2], bucket_of[0:1, bass.ds(at(gr, PG, j), 1)])

            def expand(gr, j):
                slot = j % 2
                b = t.snap(bucket[slot])
                wait(pe, "at_copied", at(gr, PG, j + 1))
                wait(pe, f"gath{j}", at(gr, 32, 32))
                wait(pe, "u_ready", at(gr, TG, 2 * j - 2))
                wait(pe, "silu_done", at(gr, PG, j - 1))
                for k in range(2):
                    h_out, z_out = (bank[slot][:, k * D:(k + 1) * D] for bank in (h_ps, z_ps))
                    for part in range(3):
                        for o, half in ((h_out, 0), (z_out, 1)):
                            t.matmul(o, onehot_t[:, slot, k, :],
                                     parts[part][:, bass.ds(b, 1), half * D:(half + 1) * D],
                                     start=(part == 0), stop=(part == 2 and half == 0))
                    last = t.matmul(z_out, ident[:, :], gathered[:, j, k, D:2 * D], start=False, stop=True)
                last.then_inc(s["expanded"], 1)

            def add_up(gr, j):
                if not there(gr):
                    return
                slot, par = j % 2, gr[1] % 2
                wait(pe, "weighted_ready", at(gr, TG, 2 * j + 2))
                wait(pe, "agg_added", at(gr, PG, j + 1))
                for k in range(2):
                    last = t.matmul(agg_ps[slot][0:NP, 0:D], weighted[:, slot, k, 0:NP],
                                    tangents[:, par, 2 * j + k, :], start=(k == 0), stop=(k == 1))
                last.then_inc(s["agg_summed"], 1)

            def pe_group(gr):
                for j in range(PG):
                    expand(gr, j)
                    turn_onehots(*pair(gr, j, 2))
                    load_bucket(*pair(gr, j, 1))
                    add_up(*pair(gr, j, -LAG))

            turn_onehots((0, 0), 0)
            turn_onehots((0, 0), 1)
            load_bucket((0, 0), 0)
            groups(pe, pe_group)
            pairs_left(add_up)

            pe.wait_ge(s["tail_agg"], 1)
            pe.wait_ge(s["mlp_in"], 32)

            def turn_sums(q):
                wait(pe, "t_sb", 2 * q)
                for c in range(2):
                    for n, b in enumerate(quad(q)):
                        last = t.transpose(turn_ps[c][:, n * NP:(n + 1) * NP], sums[0:NP, b, c * P:(c + 1) * P],
                                           ident[0:NP, 0:NP])
                last.then_inc(s["t_ps"], 1)

            turn_sums(0)
            for q in range(NQ):
                n_cols = len(quad(q)) * NP
                pe.wait_ge(s["t_sb"], 2 * q + 2)
                wait(pe, "m1_sb", 2 * q)
                for f in range(2):
                    for c in range(2):
                        last = t.matmul(z_ps[f][:, 0:n_cols], mw1[:, c, f * P:(f + 1) * P],
                                        sumT[q % 2][:, c, 0:n_cols], start=(c == 0), stop=(c == 1))
                    last.then_inc(s["m1_ps"], 1)
                if q + 1 < NQ:
                    turn_sums(q + 1)
                pe.wait_ge(s["m1_sb"], 2 * q + 2)
                for n, b in enumerate(quad(q)):
                    wait(pe, "m2_sb", b - 1)
                    for f in range(2):
                        last = t.matmul(agg_ps[b % 2][0:NP, 0:D], hidT[q % 2][:, f, n * NP:(n + 1) * NP],
                                        mw2[:, f, :], start=(f == 0), stop=(f == 1))
                    last.then_inc(s["m2_ps"], 1)

        @block.scalar
        def _(act):
            a = nc.scalar
            act.wait_ge(s["var_ready"], 1)
            a.activation(small[0:NP, 1, :], small[0:NP, 0, :], ACT.Sqrt).then_inc(s["std_ready"], 1)
            act.wait_ge(s["h_ready"], 1)
            act.wait_ge(s["base_done"], 1)
            for b in range(NB):
                wait(act, "sq_setup", b - 1)
                a.activation(square_out[0:NP, b % 2, 0:D - 1], h[:, b, 1:D], ACT.Square,
                             accum_out=small[0:NP, 2, b:b + 1]).then_inc(s["sq_setup"], 1)
            act.wait_ge(s["theta_ready"], 1)
            act.wait_ge(s["sq_setup"], NB)
            a.activation(small[0:NP, 6, :], small[0:NP, 5, :], ACT.Sqrt).then_inc(s["root_ready"], 1)
            a.activation(small[0:NP, 7, :], small[0:NP, 2, :], ACT.Sqrt).then_inc(s["root_ready"], 1)
            act.wait_ge(s["log_arg"], 1)
            a.activation(small[0:NP, 9, :], small[0:NP, 8, :], ACT.Ln).then_inc(s["log_ready"], 1)
            act.wait_ge(s["coef_ready"], 1)
            act.wait_ge(s["tails_zero"], 1)
            def scale_column(c, slot, first_use=False):
                if not first_use:
                    act.wait_ge(s["hots_used"], c + (1 - HOT))
                act.wait_ge(s["hots_built"], c * 4 + 1)
                for k in range(2, 6):
                    part = (*word_parts, *dist_terms)[k]
                    a.activation(slot_val[0:NP, slot, k, :], slot_hot[0:NP, slot, :], ACT.Copy,
                                 scale=part[:, bass.ds(c + (EC - MOVED), 1)]).then_inc(s["hots_scaled"], 1)

            def copy_turn(b):
                act.wait_ge(s["ht_ps"], b + 1)
                wait(act, "pq_ps", b - 1)
                a.activation(hT[:, b % 2, 0:2 * NP], turn_ps[b % 2][:, 0:2 * NP], ACT.Copy).then_inc(s["ht_sb"], 1)

            def second_part(b):
                act.wait_ge(s["rest_ready"], 2 * b + 2)
                a.activation(parts[1][0:NP, b, :].rearrange("p (a d) -> p a d", a=2), rest[0:NP, :, :], ACT.Copy) \
                    .then_inc(s["part1"], 1)

            copy_turn(0)
            for b in range(NB):
                if b + 1 < NB:
                    copy_turn(b + 1)
                a.activation(parts[0][0:NP, b, 0:D], h[:, b, :], ACT.Copy).then_inc(s["part0"], 1)
                if b:
                    second_part(b - 1)
                act.wait_ge(s["pq_ps"], b + 1)
                wait(act, "rest_ready", 2 * (b - 1))
                a.activation(pf[0:NP, b % 2, :], z_ps[b % 2][0:NP, 0:D], ACT.Copy,
                             scale=small[0:NP, 11, b:b + 1]).then_inc(s["pf_ready"], 1)
                act.wait_ge(s["pf_ready"], b + 1)
                a.activation(parts[0][0:NP, b, D:2 * D], pf[0:NP, b % 2, :], ACT.Copy).then_inc(s["part0"], 1)
            second_part(NB - 1)
            act.wait_ge(s["part2"], NB)
            for slot in range(HOT):
                scale_column(slot, slot, first_use=True)
            with act.Fori(1, MOVED // HOT) as i:
                for slot in range(HOT):
                    scale_column(i * HOT + slot, slot)

            def copy_turned(gr, j):
                slot = j % 2
                wait(act, "at_ready", at(gr, PG, j + 1))
                wait(act, "expanded", at(gr, PG, j - 1))
                a.activation(onehot_t[:, slot, :, :].rearrange("p k e -> p (k e)"), at_ps[slot], ACT.Copy) \
                    .then_inc(s["at_copied"], 1)

            def hidden_layer(gr, j):
                slot = j % 2
                wait(act, "expanded", at(gr, PG, j + 1))
                wait(act, "dot_done", at(gr, TG, 2 * j - 2))
                a.activation(hidden[:, slot, :, :], two(z_ps[slot]), ACT.Silu) \
                    .then_inc(s["silu_done"], 1)

            def square_tangents(gr, j):
                if not there(gr):
                    return
                par = gr[1] % 2
                for k in range(2):
                    wait(act, "u_ready", at(gr, TG, 2 * j + k + 1))
                    wait(act, "sq_done", at(gr, TG, 2 * j + k - 1))
                    a.activation(square_out[:, k, 0:D - 1], tangents[:, par, 2 * j + k, 1:D], ACT.Square,
                                 accum_out=uu[:, par, 2 * j + k:2 * j + k + 1]).then_inc(s["sq_done"], 1)

            def roots(gr):
                if not there(gr):
                    return
                asks = (
                    (2, wt[2], wt[1], ACT.Ln, -1.0, 0.0),
                    (2, wt[3], wt[2], ACT.Exp, 0.5, 0.0),
                    (5, wt[4], wt[8], ACT.Ln, 1.0, 0.0),
                    (5, wt[6], wt[4], ACT.Exp, -0.5, 0.0),
                    (5, wt[9], logit[:, gr[1] % 2, :], ACT.Exp, -1.0, nb2col[:, :]),
                    (6, wt[10], wt[5], ACT.Ln, 1.0, 0.0))
                a.preload_act_table_set("natural_log_exp_and_others")
                wait(act, "dot_done", at(gr, TG, TG))
                for n, (after, o, i, f, scale, bias) in enumerate(asks):
                    wait(act, "w_vec", at(gr, CHAIN, after))
                    if n in (1, 3):
                        wait(act, "w_act", at(gr, CHAIN_A, n))
                    a.activation(o[:, :], i if n == 4 else i[:, :], f, scale=scale, bias=bias).then_inc(s["w_act"], 1)

            def weigh_onehots(gr, j):
                if not there(gr):
                    return
                slot, par = j % 2, gr[1] % 2
                wait(act, "w_vec", at(gr, CHAIN, CHAIN))
                wait(act, "agg_summed", at(gr, PG, j - 1))
                for k in range(2):
                    a.activation(weighted[:, slot, k, 0:NP], onehot[:, par * TG + 2 * j + k, 0:NP], ACT.Copy,
                                 scale=weight[:, par, 2 * j + k:2 * j + k + 1]).then_inc(s["weighted_ready"], 1)

            def act_group(gr):
                for j in range(PG):
                    weigh_onehots(*pair(gr, j, -LAG))
                    hidden_layer(gr, j)
                    copy_turned(*pair(gr, j, 2))
                    square_tangents(*pair(gr, j, -1))
                    if j == 2:
                        roots((gr[0], gr[1] - 1))

            copy_turned((0, 0), 0)
            copy_turned((0, 0), 1)
            groups(act, act_group)
            square_tangents((0, NG - 1), PG - 1)
            roots((0, NG - 1))
            pairs_left(weigh_onehots)

            for b in range(NB):
                act.wait_ge(s["self_u"], b + 1)
                act.wait_ge(s["self_sq"], b) if b else act.wait_ge(s["sq_done"], J)
                a.activation(square_out[0:NP, 0, 0:D - 1], hidden[0:NP, b % 2, 0, 1:D], ACT.Square,
                             accum_out=small[0:NP, 17, b:b + 1]).then_inc(s["self_sq"], 1)
            n_said = [0]

            def say(o, i, f, scale=1.0):
                n_said[0] += 1
                act.wait_ge(s["tail_ask"], n_said[0])
                a.activation(small[0:NP, o, :], small[0:NP, i, :], f, scale=scale).then_inc(s["tail_say"], 1)

            say(20, 19, ACT.Sqrt, -1.0)
            say(22, 21, ACT.Ln)
            say(20, 19, ACT.Sqrt)
            for q in range(NQ):
                n_cols = len(quad(q)) * NP
                act.wait_ge(s["t_ps"], q + 1)
                wait(act, "m1_ps", 2 * (q - 1))
                for c in range(2):
                    a.activation(sumT[q % 2][:, c, 0:n_cols], turn_ps[c][:, 0:n_cols], ACT.Copy, scale=0.01) \
                        .then_inc(s["t_sb"], 1)
                for f in range(2):
                    act.wait_ge(s["m1_ps"], 2 * q + f + 1)
                    wait(act, "m2_ps", 4 * (q - 1))
                    a.activation(hidT[q % 2][:, f, 0:n_cols], z_ps[f][:, 0:n_cols], ACT.Silu,
                                 bias=mb1col[:, f:f + 1]).then_inc(s["m1_sb"], 1)
            for b in range(NB):
                act.wait_ge(s["o_ready"], b + 1)
                act.wait_ge(s["o_sq"], b) if b else None
                a.activation(square_out[0:NP, 1, 0:D - 1], sums[0:NP, b, 1:D], ACT.Square,
                             accum_out=small[0:NP, 18, b:b + 1]).then_inc(s["o_sq"], 1)
            say(4, 3, ACT.Sqrt)
            say(5, 4, ACT.Exp)
            say(6, 4, ACT.Exp, -1.0)
            for b in range(NB):
                act.wait_ge(s["y_ready"], b + 1)
                act.wait_ge(s["y_sq"], b) if b else None
                a.activation(square_out[0:NP, 1, 0:D - 1], sums[0:NP, b, 1:D], ACT.Square,
                             accum_out=small[0:NP, 13, b:b + 1]).then_inc(s["y_sq"], 1)
            say(15, 14, ACT.Sqrt)

        @block.vector
        def _(dve):
            v = nc.vector
            n = [0]

            def step(ins):
                n[0] += 1
                ins.then_inc(s["vec"], 1)
                dve.wait_ge(s["vec"], n[0])

            def sm(k, rows=NP):
                return small[0:rows, k, :]

            dve.wait_ge(s["edges_in"], 48)
            step(v.tensor_copy(src_f, src_i))
            step(v.tensor_scalar(buck, src_f, 1.0 / NP, 0.5 / NP - 0.5, ALU.mult, ALU.add))
            step(v.tensor_scalar(buck, buck, MAGIC, None, ALU.add))
            step(v.tensor_scalar(buck, buck, -MAGIC, None, ALU.add))
            step(v.scalar_tensor_tensor(local, buck, -float(NP), src_f, ALU.mult, ALU.add))
            for b in range(NB):
                step(v.tensor_scalar(ind, buck, float(b), None, ALU.is_equal, ALU.add,
                                     accum_out=counts[0:NP, b:b + 1]))
            dve.nop().then_inc(s["counted"], 1)
            step(v.memset(ones_row, 1.0))
            step(v.tensor_copy(dst_f, dst_i))
            step(v.tensor_scalar(word_parts[0], local, float(WORD), float(WORD), ALU.mult, ALU.add))
            step(v.tensor_tensor(rec_src[:, :, 0], word_parts[0], dst_f, ALU.add))
            step(v.tensor_copy(rec_src[:, :, 1], dist_in))
            dve.wait_ge(s["consts_ready"], 1)
            dve.wait_ge(s["count_ps"], 1)
            step(v.tensor_scalar(off[:, 0, :], agg_ps[1][:, 0:NB], 1.0 / PAIR, (PAIR - 1.0) / PAIR - 0.498,
                                 ALU.mult, ALU.add))
            step(v.tensor_scalar(off[:, 0, :], off[:, 0, :], MAGIC, None, ALU.add))
            step(v.tensor_scalar(off[:, 0, :], off[:, 0, :], -MAGIC, None, ALU.add))
            step(v.tensor_tensor_scan(off[:, 1, :], ones[:, 0:NB], off[:, 0, :], 0.0, ALU.mult, ALU.add))
            step(v.tensor_tensor(off[:, 2, :], off[:, 1, :], off[:, 0, :], ALU.subtract))
            step(v.scalar_tensor_tensor(off[0:NP, 3, :], off[0:NP, 2, :], float(PAIR), agg_ps[0][0:NP, 0:NB],
                                        ALU.mult, ALU.add))
            step(v.tensor_scalar(off[0:NP, 4, :], off[0:NP, 3, :], -1.0, None, ALU.add))
            dve.nop().then_inc(s["base_done"], 1)
            for b in range(NB):
                step(v.tensor_scalar(ind, buck, float(b), None, ALU.is_equal))
                step(v.tensor_tensor_scan(scan, ones_row, ind, off[0:NP, 4, b:b + 1], ALU.mult, ALU.add))
                if b == 0:
                    step(v.tensor_tensor(pos, ind, scan, ALU.mult))
                else:
                    step(v.tensor_tensor(tmp, ind, scan, ALU.mult))
                    step(v.tensor_tensor(pos, pos, tmp, ALU.add))
            step(v.tensor_copy(pos_i, pos))
            step(v.tensor_scalar(lo_i, pos_i, P - 1, None, ALU.bitwise_and))
            step(v.tensor_scalar(hi_i, pos_i, P.bit_length() - 1, None, ALU.logical_shift_right))
            step(v.tensor_copy(src_f, lo_i))
            step(v.tensor_copy(tmp, hi_i))
            step(v.scalar_tensor_tensor(pos, src_f, float(J), tmp, ALU.mult, ALU.add))
            step(v.tensor_copy(row_i, pos))
            dve.nop().then_inc(s["sort_done"], 1)
            step(v.memset(pair_acc[:, :], 0.0))
            for b in range(NB - 1):
                step(v.scalar_tensor_tensor(pair_acc[:, :], pair_iota[:, :], off[0:1, 1, b:b + 1], pair_acc[:, :],
                                            ALU.is_ge, ALU.add))
            step(v.tensor_copy(bucket_of[:, 0:NPAIR], pair_acc[:, :]))
            step(v.memset(bucket_of[:, NPAIR:NPAIR + 1], 0))
            dve.nop().then_inc(s["buckets_ready"], 1)

            dve.wait_ge(s["weights_in"], 16 * 9)
            step(v.tensor_scalar(nb2col[:, :], b2col[:, :], -1.0, None, ALU.mult))
            step(v.tensor_copy(w1c_parts[:, 0, :], w1c[:, :]))
            step(v.tensor_tensor(w1c[:, :], w1c[:, :], w1c_parts[:, 0, :], ALU.subtract))
            step(v.tensor_copy(w1c_parts[:, 1, :], w1c[:, :]))
            step(v.tensor_tensor(w1c_parts[:, 2, :], w1c[:, :], w1c_parts[:, 1, :], ALU.subtract))
            dve.nop().then_inc(s["w1c_split"], 1)

            dve.wait_ge(s["x_in"], 16)
            for b in range(NB):
                step(v.bn_stats(stats[0:NP, b % 2, :], xin[:, b, :]))
                step(v.bn_aggr(meanvar[0:NP, b, :], stats[0:NP, b % 2, :]))
            step(v.tensor_scalar(sm(0), meanvar[0:NP, :, 1], 1e-5, None, ALU.add))
            dve.nop().then_inc(s["var_ready"], 1)
            dve.wait_ge(s["std_ready"], 1)
            step(v.reciprocal(sm(3), sm(1)))
            for b in range(NB):
                step(v.tensor_scalar(h[:, b, :], xin[:, b, :], meanvar[0:NP, b, 0:1], small[0:NP, 3, b:b + 1],
                                     ALU.subtract, ALU.mult))
            step(v.tensor_scalar(h, h, 0.0, None, ALU.max))
            dve.nop().then_inc(s["h_ready"], 1)
            step(v.tensor_scalar(sm(3), h[:, :, 0], 1.0 + EPS, None, ALU.max))
            step(v.tensor_scalar(sm(4), sm(3), -1.0, None, ALU.add))
            step(v.scalar_tensor_tensor(sm(5), sm(3), 1.0, sm(4), ALU.add, ALU.mult))
            dve.nop().then_inc(s["theta_ready"], 1)
            dve.wait_ge(s["root_ready"], 2)
            step(v.tensor_tensor(sm(8), sm(6), sm(3), ALU.add))
            dve.nop().then_inc(s["log_arg"], 1)
            step(v.tensor_scalar(sm(7), sm(7), 1e-15, None, ALU.max))
            step(v.reciprocal(sm(10), sm(7)))
            dve.wait_ge(s["log_ready"], 1)
            step(v.tensor_tensor(sm(11), sm(9), sm(10), ALU.mult))
            dve.nop().then_inc(s["coef_ready"], 1)
            step(v.tensor_tensor(sm(12), h[:, :, 0], h[:, :, 0], ALU.mult))
            step(v.tensor_tensor(sm(12), sm(2), sm(12), ALU.subtract))
            step(v.tensor_scalar(sm(12), sm(12), SELF_MAX, None, ALU.min))
            shift = LOW.bit_length() - 1
            step(v.tensor_scalar(lo_i, dst_i, shift, None, ALU.logical_shift_right))
            step(v.tensor_scalar(lo_i, lo_i, shift, None, ALU.logical_shift_left))
            step(v.tensor_copy(word_parts[1], lo_i))
            step(v.tensor_tensor(word_parts[2], dst_f, word_parts[1], ALU.subtract))
            step(v.tensor_copy(rough, dist_in))
            step(v.tensor_copy(dist_terms[0], rough))
            step(v.tensor_tensor(dist_terms[2], dist_in, dist_terms[0], ALU.subtract))
            step(v.tensor_copy(rough, dist_terms[2]))
            step(v.tensor_copy(dist_terms[1], rough))
            step(v.tensor_tensor(dist_terms[2], dist_terms[2], dist_terms[1], ALU.subtract))
            dve.wait_ge(s["tile_iota"], 1)

            def build_column(c, slot, first_use=False):
                here = bass.ds(c + (EC - MOVED), 1)
                if not first_use:
                    dve.wait_ge(s["hots_used"], c + (1 - HOT))
                v.tensor_scalar(slot_hot[0:NP, slot, :], iota_b[0:NP, :], slot_f[:, here], None,
                                ALU.is_equal).then_inc(s["hots_built"], 1)
                v.tensor_scalar(tile_hot[0:NP, slot, :], tile_iota[0:NP, :], tile_f[:, here], None,
                                ALU.is_equal).then_inc(s["hots_built"], 1)
                for k in range(2):
                    v.tensor_scalar(slot_val[0:NP, slot, k, :], iota_b[0:NP, :], slot_f[:, here],
                                    word_parts[k][:, here], ALU.is_equal, ALU.mult).then_inc(s["hots_built"], 1)

            dve.wait_ge(s["tails_zero"], 1)
            dve.wait_ge(s["table_tails"], 48)
            def third_part(b):
                dve.wait_ge(s["part1"], b + 1)
                v.tensor_tensor(parts[2][0:NP, b, :].rearrange("p (a d) -> p a d", a=2), rest[0:NP, :, :],
                                parts[1][0:NP, b, :].rearrange("p (a d) -> p a d", a=2),
                                ALU.subtract).then_inc(s["part2"], 1)

            for b in range(NB):
                if b:
                    third_part(b - 1)
                dve.wait_ge(s["pq_ps"], b + 1)
                v.scalar_tensor_tensor(xin[:, b, :], h_ps[b % 2][0:NP, 0:D], small[0:NP, 11, b:b + 1],
                                       b1row[0:NP, :], ALU.mult, ALU.add).then_inc(s["q_ready"], 1)
                dve.wait_ge(s["part0"], 2 * b + 1)
                wait(dve, "part2", b)
                v.tensor_tensor(rest[0:NP, 0, :], h[:, b, :], parts[0][0:NP, b, 0:D], ALU.subtract) \
                    .then_inc(s["rest_ready"], 1)
                dve.wait_ge(s["part0"], 2 * b + 2)
                v.tensor_tensor(rest[0:NP, 1, :], pf[0:NP, b % 2, :], parts[0][0:NP, b, D:2 * D], ALU.subtract) \
                    .then_inc(s["rest_ready"], 1)
            third_part(NB - 1)
            dve.wait_ge(s["part2"], NB)
            for slot in range(HOT):
                build_column(slot, slot, first_use=True)
            with dve.Fori(1, MOVED // HOT) as i:
                for slot in range(HOT):
                    build_column(i * HOT + slot, slot)
            dve.wait_ge(s["recs_in"], 16)
            dve.wait_ge(s["hots_used"], MOVED)
            step(v.tensor_tensor(word, raw[:, :, 0], agg_ps[0][:, 0:J], ALU.add))
            step(v.tensor_copy(word_i, word))
            step(v.tensor_scalar(recs[:, 0:J, 1].bitcast(i32), word_i, WORD - 1, None, ALU.bitwise_and))
            step(v.tensor_scalar(high_i, word_i, WORD.bit_length() - 1, None, ALU.logical_shift_right))
            step(v.tensor_copy(recs[:, 0:J, 0], high_i))
            step(v.memset(recs[:, J:, :], 0.0))
            dve.nop().then_inc(s["recs_ready"], 1)
            step(v.tensor_scalar(recs[:, :, 0], recs[:, :, 0], -1.0, None, ALU.add))
            step(v.tensor_tensor(recs[:, 0:J, 2], raw[:, :, 1], agg_ps[1][:, 0:J], ALU.add))
            step(v.memset(sums[:, :, :], 0.0))
            step(v.tensor_copy(dist_parts[:, :, 0], recs[:, :, 2]))
            step(v.tensor_tensor(rest_d, recs[:, :, 2], dist_parts[:, :, 0], ALU.subtract))
            step(v.tensor_copy(dist_parts[:, :, 1], rest_d))
            step(v.tensor_tensor(dist_parts[:, :, 2], rest_d, dist_parts[:, :, 1], ALU.subtract))

            dve.nop().then_inc(s["agg_added"], 1)
            dve.nop().then_inc(s["agg_added"], 1)
            bucket = [v.alloc_register(f"dve_bucket{j}") for j in range(2)]

            def build_onehot(gr, j, k):
                ring = (gr[1] % 2) * TG + 2 * j
                wait(dve, "weighted_ready", at(gr, TG, 2 * j + 2 - 2 * TG))
                v.tensor_scalar(onehot[:, ring + k, 0:NP], iota_b[:, 0:NP],
                                recs[:, bass.ds(at(gr, TG, 2 * j + k), 1), 0], None,
                                ALU.is_equal).then_inc(s["onehots"], 1)

            def build_distance(gr, j):
                ring = (gr[1] % 2) * TG + 2 * j
                v.tensor_copy(onehot[:, ring:ring + 2, NP:P], dist_parts[:, bass.ds(at(gr, TG, 2 * j), 2), :]) \
                    .then_inc(s["onehots"], 1)

            def attention_dot(gr, j, k):
                if not there(gr):
                    return
                slot, par = j % 2, gr[1] % 2
                wait(dve, "silu_done", at(gr, PG, j + 1))
                wait(dve, "dot_done", at(gr, TG, 2 * j + k - 1))
                v.tensor_tensor_reduce(out=dot_out[:, k, :], in0=hidden[:, slot, k, :], in1=w2row[:, :],
                                       scale=1.0, scalar=0.0, op0=ALU.mult, op1=ALU.add,
                                       accum_out=logit[:, par, 2 * j + k:2 * j + k + 1]) \
                    .then_inc(s["dot_done"], 1)

            def load_bucket(gr, j):
                if there(gr):
                    v.reg_load(bucket[j % 2], bucket_of[0:1, bass.ds(at(gr, PG, j), 1)])

            def add_sums(gr, j):
                if not there(gr):
                    return
                b = v.snap(bucket[j % 2])
                wait(dve, "agg_summed", at(gr, PG, j + 1))
                wait(dve, "agg_added", at(gr, PG, j + 2))
                v.tensor_tensor(sums[0:NP, bass.ds(b, 1), :], agg_ps[j % 2][0:NP, None, 0:D],
                                sums[0:NP, bass.ds(b, 1), :], ALU.add).then_inc(s["agg_added"], 1)

            def vec_pair(gr, j):
                slot, par = j % 2, gr[1] % 2
                new, old = pair(gr, j, 3), pair(gr, j, -1)
                wait(dve, "expanded", at(gr, PG, j + 1))
                v.scalar_tensor_tensor(neg0[:, slot, :], two(h_ps[slot])[:, :, 0], -1.0,
                                       gathered[:, j, :, 0], ALU.mult, ALU.mult).then_inc(s["neg_done"], 1)
                build_onehot(*new, 0)
                build_onehot(*new, 1)
                build_distance(*new)
                wait(dve, "neg_done", at(gr, PG, j + 1))
                for k in range(2):
                    wait(dve, "mink_done", at(gr, TG, 2 * j + k - 1))
                    v.tensor_tensor_reduce(out=mink_out[:, k, 0:D - 1], in0=h_ps[slot][:, k * D + 1:(k + 1) * D],
                                           in1=gathered[:, j, k, 1:D], scale=1.0,
                                           scalar=neg0[:, slot, k:k + 1], op0=ALU.mult, op1=ALU.add,
                                           accum_out=mink[:, 2 * j + k:2 * j + k + 1]).then_inc(s["mink_done"], 1)
                attention_dot(*old, 0)
                wait(dve, "mink_done", at(gr, TG, 2 * j + 2))
                v.tensor_scalar(xy[:, par, 2 * j:2 * j + 2], mink[:, 2 * j:2 * j + 2], SELF_MAX, None,
                                ALU.min).then_inc(s["xy_done"], 1)
                attention_dot(*old, 1)
                wait(dve, "xy_done", at(gr, PG, j + 1))
                for k in range(2):
                    v.scalar_tensor_tensor(tangents[:, par, 2 * j + k, :], h_ps[slot][:, k * D:(k + 1) * D],
                                           xy[:, par, 2 * j + k:2 * j + k + 1], gathered[:, j, k, 0:D],
                                           ALU.mult, ALU.add).then_inc(s["u_ready"], 1)

            def chain(gr, n, ins):
                ins.then_inc(s["w_vec"], 1)
                wait(dve, "w_vec", at(gr, CHAIN, n))

            def to_weights(gr, stage):
                if not there(gr):
                    return
                par = gr[1] % 2
                xys = xy[:, par, :]
                if stage == 0:
                    chain(gr, 1, v.tensor_scalar(wt[0][:, :], xys, -1.0, -1.0, ALU.mult, ALU.add))
                    chain(gr, 2, v.scalar_tensor_tensor(wt[1][:, :], xys, 1.0, wt[0][:, :],
                                                        ALU.subtract, ALU.mult))
                    chain(gr, 3, v.tensor_tensor(wt[7][:, :], tangents[:, par, :, 0], tangents[:, par, :, 0],
                                                 ALU.mult))
                if stage == 1:
                    wait(dve, "sq_done", at(gr, TG, TG))
                    chain(gr, 4, v.tensor_tensor(wt[8][:, :], uu[:, par, :], wt[7][:, :], ALU.subtract))
                    chain(gr, 5, v.tensor_scalar(wt[8][:, :], wt[8][:, :], EPS, None, ALU.max))
                if stage == 2:
                    wait(dve, "w_act", at(gr, CHAIN_A, 2))
                    chain(gr, 6, v.tensor_tensor(wt[5][:, :], wt[3][:, :], xys, ALU.subtract))
                if stage == 3:
                    wait(dve, "w_act", at(gr, CHAIN_A, 5))
                    chain(gr, 7, v.tensor_scalar(wt[11][:, :], wt[9][:, :], 1.0, None, ALU.add))
                    chain(gr, 8, v.reciprocal(wt[12][:, :], wt[11][:, :]))
                    chain(gr, 9, v.tensor_tensor(wt[0][:, :], wt[12][:, :], recs[:, bass.ds(at(gr, TG, 0), TG), 2],
                                                 ALU.mult))
                    wait(dve, "w_act", at(gr, CHAIN_A, 6))
                    chain(gr, 10, v.scalar_tensor_tensor(wt[1][:, :], wt[10][:, :], ROOT50, wt[6][:, :],
                                                         ALU.min, ALU.mult))
                    chain(gr, 11, v.tensor_tensor(weight[:, par, :], wt[0][:, :], wt[1][:, :], ALU.mult))

            def vec_group(gr):
                for j in range(PG):
                    vec_pair(gr, j)
                    add_sums(*pair(gr, j, -LAG - 1))
                    load_bucket(*pair(gr, j, -LAG))
                    if j < 4:
                        to_weights((gr[0], gr[1] - 1), j)

            for j in range(3):
                for k in range(2):
                    build_onehot((0, 0), j, k)
                build_distance((0, 0), j)
            groups(dve, vec_group)
            add_sums(*pair((0, NG - 1), PG - 1, -LAG))
            for k in range(2):
                attention_dot((0, NG - 1), PG - 1, k)
            for stage in range(4):
                to_weights((0, NG - 1), stage)

            def last_sums(gr, j):
                load_bucket(gr, j)
                add_sums(gr, j)

            pairs_left(last_sums)

            dve.wait_ge(s["h_back"], 16)
            dve.wait_ge(s["agg_added"], NPAIR + 2)
            step(v.tensor_scalar(sm(14), h[:, :, 0], EPS, None, ALU.max))
            step(v.reciprocal(sm(0), sm(14)))
            for b in range(NB):
                step(v.tensor_tensor_reduce(out=mink_out[0:NP, 0, 0:D - 1], in0=h[:, b, 1:D], in1=sums[0:NP, b, 1:D],
                                            scale=1.0, scalar=0.0, op0=ALU.mult, op1=ALU.add,
                                            accum_out=small[0:NP, 16, b:b + 1]))
            step(v.tensor_tensor(sums[0:NP, :, 0], sm(16), sm(0), ALU.mult))
            dve.nop().then_inc(s["tail_agg"], 1)
            for b in range(NB):
                wait(dve, "self_sq", b - 1)
                v.scalar_tensor_tensor(hidden[0:NP, b % 2, 0, :], h[:, b, :], small[0:NP, 12, b:b + 1], h[:, b, :],
                                       ALU.mult, ALU.add).then_inc(s["self_u"], 1)
            dve.wait_ge(s["self_sq"], NB)

            asked = [0]

            def ask():
                asked[0] += 1
                dve.nop().then_inc(s["tail_ask"], 1)
                dve.wait_ge(s["tail_say"], asked[0])

            step(v.tensor_tensor(sm(1), h[:, :, 0], sm(12), ALU.mult))
            step(v.tensor_tensor(sm(1), sm(1), h[:, :, 0], ALU.add))
            step(v.tensor_tensor(sm(1), sm(1), sm(1), ALU.mult))
            step(v.tensor_tensor(sm(2), sm(17), sm(1), ALU.subtract))
            step(v.tensor_scalar(sm(2), sm(2), EPS, None, ALU.max))
            step(v.reciprocal(sm(3), sm(2)))
            step(v.tensor_scalar(sm(4), sm(12), -1.0, -1.0, ALU.mult, ALU.add))
            step(v.scalar_tensor_tensor(sm(19), sm(12), 1.0, sm(4), ALU.subtract, ALU.mult))
            ask()
            step(v.tensor_tensor(sm(21), sm(20), sm(12), ALU.subtract))
            ask()
            step(v.tensor_tensor(sm(5), sm(22), sm(22), ALU.mult))
            step(v.scalar_tensor_tensor(sm(19), sm(5), 50.0, sm(3), ALU.min, ALU.mult))
            ask()
            for b in range(NB):
                dve.wait_ge(s["m2_ps"], b + 1)
                step(v.tensor_tensor(sums[0:NP, b, :], agg_ps[b % 2][0:NP, 0:D], mb2row[0:NP, :], ALU.add))
                dve.nop().then_inc(s["m2_sb"], 1)
                step(v.scalar_tensor_tensor(hidden[0:NP, 0, 1, :], h[:, b, :], small[0:NP, 12, b:b + 1], h[:, b, :],
                                            ALU.mult, ALU.add))
                step(v.scalar_tensor_tensor(sums[0:NP, b, :], hidden[0:NP, 0, 1, :], small[0:NP, 20, b:b + 1],
                                            sums[0:NP, b, :], ALU.mult, ALU.add))
                dve.nop().then_inc(s["o_ready"], 1)
                step(v.tensor_tensor_reduce(out=mink_out[0:NP, 0, 0:D - 1], in0=h[:, b, 1:D], in1=sums[0:NP, b, 1:D],
                                            scale=1.0, scalar=0.0, op0=ALU.mult, op1=ALU.add,
                                            accum_out=small[0:NP, 16, b:b + 1]))
            dve.wait_ge(s["o_sq"], NB)
            step(v.tensor_tensor(sm(1), sm(16), sm(0), ALU.mult))
            step(v.tensor_tensor(sm(2), sm(1), sm(1), ALU.mult))
            step(v.tensor_tensor(sm(3), sm(18), sm(2), ALU.subtract))
            step(v.tensor_scalar(sm(3), sm(3), EPS, None, ALU.max))
            ask()
            step(v.tensor_scalar(sm(4), sm(4), 1e6, 1e-15, ALU.min, ALU.max))
            ask()
            ask()
            step(v.tensor_tensor(sm(7), sm(5), sm(6), ALU.add))
            step(v.tensor_scalar(sm(7), sm(7), 0.5, None, ALU.mult))
            step(v.tensor_tensor(sm(8), sm(5), sm(6), ALU.subtract))
            step(v.reciprocal(sm(9), sm(4)))
            step(v.scalar_tensor_tensor(sm(8), sm(8), 0.5, sm(9), ALU.mult, ALU.mult))
            step(v.tensor_tensor(sm(9), sm(4), sm(4), ALU.mult))
            step(v.tensor_scalar(sm(9), sm(9), 1.0, None, ALU.min))
            step(v.tensor_scalar(sm(10), sm(4), 1.0, None, ALU.is_lt))
            step(v.tensor_scalar(sm(11), sm(4), 1.0, None, ALU.is_ge))
            for o, terms in ((21, (90.0, 56.0, 30.0, 12.0, 2.0)), (22, (110.0, 72.0, 42.0, 20.0, 6.0))):
                step(v.tensor_scalar(sm(o), sm(9), 1.0 / terms[0], 1.0, ALU.mult, ALU.add))
                for term in terms[1:]:
                    step(v.tensor_tensor(sm(o), sm(o), sm(9), ALU.mult))
                    step(v.tensor_scalar(sm(o), sm(o), 1.0 / term, 1.0, ALU.mult, ALU.add))
            for e, o in ((7, 21), (8, 22)):
                step(v.tensor_tensor(sm(e), sm(e), sm(11), ALU.mult))
                step(v.tensor_tensor(sm(o), sm(o), sm(10), ALU.mult))
                step(v.tensor_tensor(sm(e), sm(e), sm(o), ALU.add))
            for b in range(NB):
                step(v.tensor_scalar(sums[0:NP, b, :], sums[0:NP, b, :], small[0:NP, 8, b:b + 1], None, ALU.mult))
                step(v.scalar_tensor_tensor(sums[0:NP, b, :], h[:, b, :], small[0:NP, 7, b:b + 1], sums[0:NP, b, :],
                                            ALU.mult, ALU.add))
                dve.nop().then_inc(s["y_ready"], 1)
            dve.wait_ge(s["y_sq"], NB)
            step(v.tensor_scalar(sm(14), sm(13), 1.0, None, ALU.add))
            ask()
            step(v.tensor_copy(sums[0:NP, :, 0], sm(15)))
            dve.wait_ge(s["x_back"], 16)
            step(v.tensor_tensor(xin, xin, sums[0:NP, :, :], ALU.add))
            dve.nop().then_inc(s["out_ready"], 1)


_INS = ["x", "src", "dst", "edge_weight1", "L0_gnn_att_w1", "L0_gnn_att_b1", "L0_gnn_att_w2", "L0_gnn_att_b2",
        "L0_gnn_mlp_w1", "L0_gnn_mlp_b1", "L0_gnn_mlp_w2", "L0_gnn_mlp_b2"]


def kernel(**inputs):
    import numpy as _np
    import concourse.bacc as _bacc
    from concourse import mybir as _mybir
    from concourse.bass_utils import run_bass_kernel_spmd as _run

    nc = _bacc.Bacc("TRN2", target_bir_lowering=False, num_devices=1)
    arrays, args = {}, []
    for name in _INS:
        a = _np.ascontiguousarray(inputs[name])
        if name == "edge_weight1":
            a = a.reshape(-1)
        arrays[f"in_{name}_dram"] = a
        args.append(nc.dram_tensor(f"in_{name}_dram", a.shape, _mybir.dt.from_np(a.dtype), kind="ExternalInput").ap())
    shape = inputs["x"].shape
    args.append(nc.dram_tensor("out_0_dram", shape, _mybir.dt.from_np(_np.dtype("float32")),
                               kind="ExternalOutput").ap())
    hyperbolic_gnn_layer(nc, *args)
    r = _run(nc, [arrays], core_ids=[0])
    return r.results[0]["out_0_dram"]
```

```python
import concourse.bass as bass
from concourse import mybir
from contextlib import ExitStack


def hyperbolic_gnn_layer(nc, x, src, dst, dist, att_w1, att_b1, att_w2, att_b2,
                         mlp_w1, mlp_b1, mlp_w2, mlp_b2, out):
    fp32 = mybir.dt.float32
    bf16 = mybir.dt.bfloat16
    i32 = mybir.dt.int32
    ALU = mybir.AluOpType
    ACT = mybir.ActivationFunctionType

    N, D = x.shape
    E = src.shape[0]
    P = 128
    NP = 125
    NB = N // NP
    EC = E // NP
    PAIR = 2 * P
    TG = 16
    PG = TG // 2
    LAG = 12
    NPAIR = (E + NB * (PAIR - 1)) // PAIR
    NG = -(-NPAIR // PG)
    assert NB * NP == N and EC * NP == E and NG % 2 == 1
    NPAIR = NG * PG
    J = 2 * NPAIR
    EPS = 1e-7
    SELF_MAX = -1.0000001
    MAGIC = 12582912.0
    NQ = -(-NB // 4)
    CHAIN = 11
    CHAIN_A = 6
    SC = 19
    MOVED = 160
    HOT = 4
    assert MOVED % HOT == 0
    SCATTERS = (EC - MOVED) // SC
    SC_LEFT = EC - MOVED - SCATTERS * SC
    LOW = 64
    WORD = 4096
    assert N < WORD
    ROOT50 = 50.0 ** 0.5

    sorted_dram = nc.dram_tensor("sorted_edges", (P * J, 2), fp32).ap()
    node_dram = nc.dram_tensor("node_rows", (N, 2 * D), fp32).ap()

    ctx = ExitStack()
    with ctx:
        def sb(name, shape, dt=fp32):
            return ctx.enter_context(nc.sbuf_tensor(name, shape, dt))

        def pb(name, shape, dt=fp32):
            return ctx.enter_context(nc.psum_tensor(name, shape, dt))

        def sem(name):
            return ctx.enter_context(nc.semaphore(name))

        parts = [sb(f"node_part{k}", [P, NB, 2 * D], bf16) for k in range(3)]
        sums = sb("sums", [P, NB, D])
        gathered = sb("gathered", [P, PG, 2, 2 * D])
        tangents = sb("tangents", [P, 2, TG, D])
        recs = sb("recs", [P, J + 6, 4])
        dist_parts = sb("dist_parts", [P, J + 6, 3], bf16)
        onehot = sb("onehot", [P, 2 * TG, P], bf16)
        onehot_t = sb("onehot_t", [P, 2, 2, P], bf16)
        weighted = sb("weighted", [P, 2, 2, P])
        hidden = sb("hidden", [P, 2, 2, D])
        dot_out = sb("dot_out", [P, 2, D], bf16)
        mink_out = sb("mink_out", [P, 2, D], bf16)
        square_out = sb("square_out", [P, 2, D], bf16)
        ident = sb("ident", [P, P])
        ident_b = sb("ident_b", [P, P], bf16)
        iota_f = sb("iota_f", [P, P])
        iota_b = sb("iota_b", [P, P], bf16)
        ones = sb("ones", [P, P])
        before = sb("before", [P, P])
        w2row = sb("w2row", [P, D])
        mb2row = sb("mb2row", [P, D])
        mb1col = sb("mb1col", [P, 2])
        b2col = sb("b2col", [P, 1])
        nb2col = sb("nb2col", [P, 1])
        idx_now = sb("idx_now", [P, PG, 2], i32)
        bucket_of = sb("bucket_of", [1, NPAIR + 1], i32)
        neg0 = sb("neg0", [P, 2, 2])
        mink = sb("mink", [P, TG])
        xy = sb("xy", [P, 2, TG])
        uu = sb("uu", [P, 2, TG])
        logit = sb("logit", [P, 2, TG])
        wt = [sb(f"wt{k}", [P, TG]) for k in range(13)]
        weight = sb("weight", [P, 2, TG])
        small = sb("small", [P, 24, NB])
        counts = sb("counts", [P, NB])
        off = sb("off", [P, 5, NB])

        sort = sums[:, :, :].rearrange("p b d -> p (b d)")

        def col(k):
            return sort[0:NP, k * EC:(k + 1) * EC]

        src_i = col(0).bitcast(i32)
        dst_i = col(1).bitcast(i32)
        dist_in = col(2)
        src_f, buck, local, pos = (col(k) for k in range(3, 7))
        tmp = col(9)
        scans = (col(7), col(8), weighted[0:NP, :, :, :].rearrange("p a k m -> p (a k m)")[:, 0:EC])
        picks = (col(9), col(0))
        inds = [parts[0][0:NP, :, :].rearrange("p b d -> p (b d)")[:, b * EC:(b + 1) * EC] for b in range(NB)]
        pos_i, lo_i, hi_i, row_i = (col(k).bitcast(i32) for k in (0, 7, 8, 0))
        ones_row = col(14)
        rec_src = sort[0:NP, 10 * EC:12 * EC].rearrange("p (t c) -> p t c", c=2)
        slot_f, tile_f = src_f, tmp
        word_parts = (col(12), col(14), col(13))
        dst_f = col(13)
        dist_terms = (col(4), col(5), col(6))
        rough = col(7).bitcast(bf16)[:, 0:EC]
        flat_recs = recs[:, :, :].rearrange("p j c -> p (j c)")
        tile_iota = flat_recs[:, 0:J]
        tile_hot = flat_recs[:, J:J + HOT * J // 2].bitcast(bf16).rearrange("p (a j) -> p a j", a=HOT)
        slot_hot = onehot[:, 0:HOT, :]
        slot_val = onehot[:, HOT:7 * HOT, :].rearrange("p (a k) m -> p a k m", a=HOT)
        raw = sort[:, 0:2 * J].rearrange("p (j c) -> p j c", c=2)
        word = sort[:, 2 * J:3 * J]
        word_i, high_i = (sort[:, k * J:(k + 1) * J].bitcast(i32) for k in (3, 4))
        xin = tangents[0:NP, :, :, :].rearrange("p a t d -> p (a t) d")[:, 0:NB, :]
        w1 = tangents[:, :, :, :].rearrange("p a t d -> p (a t d)")[:, NB * D:NB * D + 4 * D] \
            .rearrange("p (c d) -> p c d", c=2)
        h = gathered[0:NP, :, :, :].rearrange("p j k d -> p (j k d)")[:, 0:NB * D] \
            .rearrange("p (b d) -> p b d", d=D)
        self_u = weighted[0:NP, :, :, :].rearrange("p a k m -> p a (k m)")
        hT = hidden[:, :, :, :].rearrange("p a i d -> p a (i d)")
        spare = onehot[:, :, :].rearrange("p t n -> p (t n)").bitcast(fp32)
        pf, rest = (spare[:, 2 * k * D:2 * (k + 1) * D].rearrange("p (a d) -> p a d", a=2) for k in range(2))
        w1c = spare[:, 4 * D:5 * D]
        b1row = spare[:, 5 * D:6 * D]
        w1c_parts = onehot[:, :, :].rearrange("p t n -> p (t n)")[:, 12 * D:15 * D].rearrange("p (k d) -> p k d", k=3)
        rest_d = hidden[:, :, :, :].rearrange("p a k d -> p (a k d)")[:, 0:J + 6]
        pair_iota = sb("pair_iota", [1, NPAIR])
        pair_acc = sb("pair_acc", [1, NPAIR])
        slot_idx = sb("slot_idx", [P, 2, SC], i32)
        slot_rec = sb("slot_rec", [P, 2, SC, 2])

        def quad_buffers(k):
            flat = parts[1][:, :, :].rearrange("p b d -> p (b d)").bitcast(fp32)
            return [flat[:, i * 1024:(i + 1) * 1024].rearrange("p (c n) -> p c n", c=2)
                    for i in range(2 * k, 2 * k + 2)]

        sumT, hidT = quad_buffers(0), quad_buffers(1)
        self_tangents = parts[0][0:NP, :, :].rearrange("p b d -> p (b d)").bitcast(fp32) \
            .rearrange("p (b d) -> p b d", d=D)

        mw1, mw2 = (parts[2][:, 4 * k:4 * k + 2, :].rearrange("p b d -> p (b d)").bitcast(fp32)
                    .rearrange("p (c d) -> p c d", c=2)[:, :, 0:D] for k in range(2))

        def quad(q):
            return range(4 * q, min(NB, 4 * q + 4))

        CHUNKS = (range(0, 10), range(10, 18), range(18, NB))

        def order(chunk):
            return [b for even in chunk[::2] for b in (even + 1, even) if b < chunk.stop]

        h_ps, z_ps, turn_ps, agg_ps = ([pb(f"{name}_ps{k}", [P, 2 * D]) for k in range(2)]
                                       for name in ("h", "z", "turn", "agg"))
        at_ps = [t[:, 0:P].bitcast(bf16) for t in turn_ps]

        def two(bank):
            return bank[:, :].rearrange("p (k d) -> p k d", k=2)

        s = {}
        for name in (
                "edges_in", "weights_in", "x_in", "mlp_in",
                "consts_ready", "pool_step", "pool_turn", "defaults", "w1_zeroed", "w1c_split",
                "table_zeros", "table_tails",
                "fill_out", "vec", "counted", "count_ps", "sort_done", "slot_filled",
                "scattered0", "scattered1", "recs_in", "tile_iota",
                "hots_built", "hots_scaled", "hots_used", "recs_ready",
                "sort_over", "sums_zero", "base_done",
                "x_summed", "x_squared", "x_centred", "var_ready", "std_ready", "rstd_ready",
                "h_ready", "sq_setup", "theta_ready", "root_ready",
                "log_arg", "log_ready", "coef_ready", "ht_ps", "ht_sb", "pq_ps", "pf_ready",
                "part0", "rest_ready", "part1", "part2", "q_ready", "h_out", "q_out",
                "buckets_ready", "idx_ready", *(f"gath{j}" for j in range(PG)), "onehots", "at_ready",
                "at_copied", "expanded", "silu_done", "neg_done", "mink_done", "xy_done",
                "u_ready", "sq_done", "dot_done", "w_vec", "w_act", "weighted_ready",
                "agg_summed", "agg_added", "h_back", "x_back", "tail_agg", "self_u", "self_sq",
                "tail_ask", "tail_say", "t_ps", "t_sb", "m1_ps", "m1_sb", "m2_ps",
                "o_ready", "o_dot", "h_used", "o_sq", "y_begin", "y_scaled", "y_even",
                "y_ready", "y_sq", "out_ready", "out_done"):
            s[name] = sem(name)

        def wait(eng, name, value):
            if not (isinstance(value, int) and value <= 0):
                eng.wait_ge(s[name], value)

        block = ctx.enter_context(nc.Block())

        def groups(eng, body):
            for g in range(3):
                body((0, g))
            with eng.Fori(1, (NG - 1) // 2) as i:
                body((i, 1))
                body((i, 2))

        def at(g, per, plus):
            i, o = g
            return per * o + plus if isinstance(i, int) else i * (2 * per) + (per * o + plus)

        def pair(g, j, n):
            return (g[0], g[1] + (j + n) // PG), (j + n) % PG

        def there(g):
            return not (isinstance(g[0], int) and g[1] < 0)

        def pairs_left(per_pair, lag):
            for n in range(lag):
                per_pair(*pair((0, NG - 1), PG - lag, n))

        @block.sync
        def _(sp):
            for a, d in ((src, src_i), (dst, dst_i), (dist, dist_in)):
                sp.dma_start(d, a.rearrange("(p t) -> p t", p=NP)).then_inc(s["edges_in"], 16)
            sp.dma_start(xin, x.rearrange("(b l) d -> l b d", l=NP)).then_inc(s["x_in"], 16)
            for half in range(2):
                sp.dma_start(w1[:, :, half * D:(half + 1) * D],
                             att_w1[half * D:(half + 1) * D, :].rearrange("(c p) d -> p c d", p=P)) \
                    .then_inc(s["weights_in"], 16)
            for a, d in ((att_w1[2 * D:2 * D + 1, :], w1c), (att_b1[None, :], b1row),
                         (att_w2.rearrange("d o -> o d"), w2row), (mlp_b2[None, :], mb2row)):
                sp.dma_start(d[:, :], a.broadcast_to((P, D))).then_inc(s["weights_in"], 16)
            for c in range(2):
                sp.dma_start(mb1col[:, c:c + 1], mlp_b1[c * P:(c + 1) * P][:, None]).then_inc(s["weights_in"], 16)
            sp.dma_start(b2col[:, :], att_b2[None, :].broadcast_to((P, 1))).then_inc(s["weights_in"], 16)
            sp.wait_ge(s["defaults"], 1)
            sp.dma_start(sorted_dram.rearrange("(p j) c -> p (j c)", p=P),
                         flat_recs[:, 0:2 * J]).then_inc(s["fill_out"], 16)
            for k in range(3):
                sp.dma_start(parts[k][NP:P, :, 0:D],
                             flat_recs[NP:P, None, J * 3:J * 3 + D // 2].bitcast(bf16).broadcast_to((P - NP, NB, D))) \
                    .then_inc(s["table_zeros"], 16)
            sp.wait_ge(s["w1c_split"], 1)
            for k in range(3):
                sp.dma_start(parts[k][NP:P, :, D:2 * D],
                             w1c_parts[NP:P, k, None, :].broadcast_to((P - NP, NB, D))).then_inc(s["table_tails"], 16)
            rows = node_dram.rearrange("(b l) d -> l b d", l=NP)
            sp.wait_ge(s["h_ready"], NB)
            sp.dma_start(rows[:, :, 0:D], h).then_inc(s["h_out"], 16)
            sp.wait_ge(s["q_ready"], NB)
            sp.dma_start(rows[:, :, D:2 * D], xin).then_inc(s["q_out"], 16)
            for slot in range(2):
                sp.wait_ge(s[f"scattered{slot}"],
                           16 * (SC * ((SCATTERS + 1 - slot) // 2) + (SC_LEFT if SCATTERS % 2 == slot else 0)))
            sp.wait_ge(s["hots_built"], 4 * MOVED)
            sp.wait_ge(s["hots_scaled"], 4 * MOVED)
            sp.dma_start(raw.rearrange("p j c -> p (j c)"),
                         sorted_dram.rearrange("(p j) c -> p (j c)", p=P)).then_inc(s["recs_in"], 16)
            sp.wait_ge(s["expanded"], NPAIR)
            sp.wait_ge(s["u_ready"], J)
            sp.dma_start(h, rows[:, :, 0:D]).then_inc(s["h_back"], 16)
            for a, d in ((mlp_w1, mw1), (mlp_w2, mw2)):
                sp.dma_start(d, a.rearrange("(c p) d -> p c d", p=P)).then_inc(s["mlp_in"], 16)
            sp.wait_ge(s["agg_summed"], NPAIR)
            sp.wait_ge(s["sq_done"], J)
            sp.dma_start(xin, x.rearrange("(b l) d -> l b d", l=NP)).then_inc(s["x_back"], 16)
            for n, chunk in enumerate(CHUNKS):
                sp.wait_ge(s["out_ready"], n + 1)
                sp.dma_start(out[chunk.start * NP:chunk.stop * NP, :].rearrange("(b l) d -> l b d", l=NP),
                             xin[:, chunk.start:chunk.stop, :]).then_inc(s["out_done"], 16)
            sp.wait_ge(s["out_done"], 16 * len(CHUNKS))

        @block.gpsimd
        def _(pool):
            n = [0]

            def step(ins):
                n[0] += 1
                ins.then_inc(s["pool_step"], 1)
                pool.wait_ge(s["pool_step"], n[0])

            g = nc.gpsimd
            step(g.memset(recs[:, :, :], 0.0))
            pool.nop().then_inc(s["defaults"], 1)
            step(g.memset(ones[:, :], 1.0))
            step(g.affine_select(out=ident[:, :], in_=ones[:, :], compare_op=ALU.is_equal, fill=0.0, base=0,
                                 pattern=[[-1, P]], channel_multiplier=1))
            step(g.affine_select(out=before[:, :], in_=ones[:, :], compare_op=ALU.is_gt, fill=0.0, base=0,
                                 pattern=[[1, P]], channel_multiplier=-1))
            step(g.tensor_copy(ident_b[:, :], ident[:, :]))
            step(g.iota(pair_iota[:, :], pattern=[[1, NPAIR]], base=0, channel_multiplier=0,
                        allow_small_or_imprecise_dtypes=True))
            step(g.iota(iota_f[:, :], pattern=[[1, P]], base=0, channel_multiplier=0,
                        allow_small_or_imprecise_dtypes=True))
            step(g.tensor_copy(iota_b[:, :], iota_f[:, :]))
            pool.nop().then_inc(s["consts_ready"], 1)
            pool.wait_ge(s["weights_in"], 16 * 9)
            g.memset(w1[0:1, 0, :], 0.0).then_inc(s["w1_zeroed"], 1)
            pool.wait_ge(s["sort_done"], 1)
            pool.wait_ge(s["fill_out"], 16)
            pool.wait_ge(s["table_zeros"], 48)
            g.iota(tile_iota, pattern=[[1, J]], base=0, channel_multiplier=0,
                   allow_small_or_imprecise_dtypes=True).then_inc(s["tile_iota"], 1)

            def scatter(i, slot, first_use, count, cols=SC):
                base = i * (2 * SC) + slot * SC
                if not first_use:
                    pool.wait_ge(s[f"scattered{slot}"], count * (16 * SC))
                g.tensor_copy(slot_idx[0:NP, slot, 0:cols], row_i[:, bass.ds(base, cols)]).then_inc(s["slot_filled"], 1)
                g.tensor_copy(slot_rec[0:NP, slot, 0:cols, :], rec_src[:, bass.ds(base, cols), :]).then_inc(s["slot_filled"], 1)
                pool.wait_ge(s["slot_filled"], i * 4 + 2 * slot + 2)
                pool.nop().then_inc(s["pool_turn"], 1)
                for c in range(cols):
                    g.indirect_dma_start(sorted_dram,
                                         bass.IndirectOffsetOnAxis(ap=slot_idx[0:NP, slot, c:c + 1], axis=0),
                                         slot_rec[0:NP, slot, c, :], None).then_inc(s[f"scattered{slot}"], 16)

            steps = SCATTERS
            scatter(0, 0, True, 0)
            scatter(0, 1, True, 0)
            with pool.Fori(1, steps // 2) as i:
                scatter(i, 0, False, i)
                scatter(i, 1, False, i)
            if steps % 2:
                scatter(steps // 2, 0, False, steps // 2)
            if SC_LEFT:
                scatter(steps // 2, steps % 2, False, steps // 2, SC_LEFT)

            pool.wait_ge(s["recs_ready"], 1)
            pool.wait_ge(s["h_out"], 16)
            pool.wait_ge(s["q_out"], 16)
            pool.wait_ge(s["part2"], NB)
            pool.wait_ge(s["sq_setup"], NB)
            pool.wait_ge(s["h_used"], 1)
            dst_of = recs[:, :, 1].bitcast(i32)

            def gather(gr):
                for j in range(PG):
                    wait(pool, "expanded", at(gr, PG, j + 1 - PG))
                    wait(pool, "u_ready", at(gr, TG, 2 * j + 2 - TG))
                    g.tensor_copy(idx_now[:, j, :], dst_of[:, bass.ds(at(gr, TG, 2 * j), 2)]) \
                        .then_inc(s["idx_ready"], 1)
                    pool.wait_ge(s["idx_ready"], at(gr, PG, j + 1))
                    pool.nop().then_inc(s["pool_turn"], 1)
                    for k in range(2):
                        g.indirect_dma_start(gathered[:, j, k, :], None, node_dram,
                                             bass.IndirectOffsetOnAxis(ap=idx_now[:, j, k:k + 1], axis=0)) \
                            .then_inc(s[f"gath{j}"], 16)

            groups(pool, gather)

        @block.tensor
        def _(pe):
            t = nc.tensor
            pe.wait_ge(s["consts_ready"], 1)
            pe.wait_ge(s["counted"], 1)
            t.matmul(agg_ps[0][0:NP, 0:NB], before[0:NP, 0:NP], counts[0:NP, :], start=True, stop=True)
            t.matmul(agg_ps[1][:, 0:NB], ones[0:NP, :], counts[0:NP, :], start=True, stop=True).then_inc(s["count_ps"], 1)
            pe.wait_ge(s["weights_in"], 16 * 9)
            pe.wait_ge(s["h_ready"], NB)
            pe.wait_ge(s["w1_zeroed"], 1)

            def turn(b):
                wait(pe, "ht_sb", b - 1)
                for c in range(2):
                    last = t.transpose(turn_ps[b % 2][:, c * NP:(c + 1) * NP], h[:, b, c * P:(c + 1) * P],
                                       ident[0:NP, 0:NP])
                last.then_inc(s["ht_ps"], 1)

            def move_column(c, slot, first=False, last=False):
                pe.wait_ge(s["hots_built"], c * 4 + 4)
                pe.wait_ge(s["hots_scaled"], c * 4 + 4)
                for k in range(6):
                    ins = t.matmul(agg_ps[k // 3][:, 0:J], slot_val[0:NP, slot, k, :], tile_hot[0:NP, slot, :],
                                   start=(first and k % 3 == 0), stop=(last and k % 3 == 2))
                ins.then_inc(s["hots_used"], 1)

            turn(0)
            for b in range(NB):
                if b + 1 < NB:
                    turn(b + 1)
                pe.wait_ge(s["ht_sb"], b + 1)
                wait(pe, "pf_ready", b - 1)
                wait(pe, "q_ready", b - 1)
                for bank, half in ((z_ps, 0), (h_ps, 1)):
                    for c in range(2):
                        last = t.matmul(bank[b % 2][0:NP, 0:D], hT[:, b % 2, c * NP:(c + 1) * NP],
                                        w1[:, c, half * D:(half + 1) * D], start=(c == 0), stop=(c == 1))
                last.then_inc(s["pq_ps"], 1)
            for slot in range(HOT):
                move_column(slot, slot, first=(slot == 0))
            with pe.Fori(1, MOVED // HOT - 1) as i:
                for slot in range(HOT):
                    move_column(i * HOT + slot, slot)
            for slot in range(HOT):
                move_column(MOVED - HOT + slot, slot, last=(slot == HOT - 1))

            bucket = [t.alloc_register(f"pe_bucket{j}") for j in range(2)]
            pe.wait_ge(s["buckets_ready"], 1)
            pe.wait_ge(s["part2"], NB)
            pe.wait_ge(s["table_zeros"], 48)
            pe.wait_ge(s["table_tails"], 48)
            pe.wait_ge(s["sq_setup"], NB)

            def turn_onehots(gr, j):
                slot, ring = j % 2, (gr[1] % 2) * TG + 2 * j
                wait(pe, "onehots", at(gr, 3 * PG, 3 * j + 3))
                wait(pe, "at_copied", at(gr, PG, j - 1))
                for k in range(2):
                    last = t.transpose(at_ps[slot][:, k * P:(k + 1) * P], onehot[:, ring + k, :], ident_b[:, :])
                last.then_inc(s["at_ready"], 1)

            def load_bucket(gr, j):
                t.reg_load(bucket[j % 2], bucket_of[0:1, bass.ds(at(gr, PG, j), 1)])

            def expand(gr, j):
                slot = j % 2
                b = t.snap(bucket[slot])
                wait(pe, "at_copied", at(gr, PG, j + 1))
                wait(pe, f"gath{j}", at(gr, 32, 32))
                wait(pe, "u_ready", at(gr, TG, 2 * j - 2))
                wait(pe, "silu_done", at(gr, PG, j - 1))
                for k in range(2):
                    t.matmul(z_ps[slot][:, k * D:(k + 1) * D], ident[:, :], gathered[:, j, k, D:2 * D],
                             start=True, stop=False)
                    for part in range(3):
                        for bank, half in ((h_ps, 0), (z_ps, 1)):
                            last = t.matmul(bank[slot][:, k * D:(k + 1) * D], onehot_t[:, slot, k, :],
                                            parts[part][:, bass.ds(b, 1), half * D:(half + 1) * D],
                                            start=(part == 0 and half == 0), stop=(part == 2))
                last.then_inc(s["expanded"], 1)

            def add_up(gr, j):
                if not there(gr):
                    return
                slot, par = j % 2, gr[1] % 2
                wait(pe, "weighted_ready", at(gr, TG, 2 * j + 2))
                wait(pe, "agg_added", at(gr, PG, j + 1))
                for k in range(2):
                    last = t.matmul(agg_ps[slot][0:NP, 0:D], weighted[:, slot, k, 0:NP],
                                    tangents[:, par, 2 * j + k, :], start=(k == 0), stop=(k == 1))
                last.then_inc(s["agg_summed"], 1)

            def pe_group(gr):
                for j in range(PG):
                    expand(gr, j)
                    turn_onehots(*pair(gr, j, 2))
                    load_bucket(*pair(gr, j, 1))
                    add_up(*pair(gr, j, -LAG - 1))

            turn_onehots((0, 0), 0)
            turn_onehots((0, 0), 1)
            load_bucket((0, 0), 0)
            groups(pe, pe_group)
            pairs_left(add_up, LAG + 1)

            pe.wait_ge(s["mlp_in"], 32)

            def turn_sums(q):
                pe.wait_ge(s["tail_agg"], q + 1)
                wait(pe, "t_sb", 2 * q)
                for c in range(2):
                    for n, b in enumerate(quad(q)):
                        last = t.transpose(turn_ps[c][:, n * NP:(n + 1) * NP], sums[0:NP, b, c * P:(c + 1) * P],
                                           ident[0:NP, 0:NP])
                last.then_inc(s["t_ps"], 1)

            turn_sums(0)
            for q in range(NQ):
                n_cols = len(quad(q)) * NP
                pe.wait_ge(s["t_sb"], 2 * q + 2)
                wait(pe, "m1_sb", 2 * q)
                for f in range(2):
                    for c in range(2):
                        last = t.matmul(z_ps[f][:, 0:n_cols], mw1[:, c, f * P:(f + 1) * P],
                                        sumT[q % 2][:, c, 0:n_cols], start=(c == 0), stop=(c == 1))
                    last.then_inc(s["m1_ps"], 1)
                if q + 1 < NQ:
                    turn_sums(q + 1)
                pe.wait_ge(s["m1_sb"], 2 * q + 2)
                for n, b in enumerate(quad(q)):
                    wait(pe, "o_ready", b - 1)
                    for f in range(2):
                        last = t.matmul(agg_ps[b % 2][0:NP, 0:D], hidT[q % 2][:, f, n * NP:(n + 1) * NP],
                                        mw2[:, f, :], start=(f == 0), stop=(f == 1))
                    last.then_inc(s["m2_ps"], 1)

        @block.scalar
        def _(act):
            a = nc.scalar
            act.wait_ge(s["x_in"], 16)
            for b in range(NB):
                wait(act, "x_summed", b - 1)
                a.activation(square_out[0:NP, b % 2, :], xin[:, b, :], ACT.Copy,
                             accum_out=small[0:NP, 13, b:b + 1]).then_inc(s["x_summed"], 1)
            act.wait_ge(s["x_summed"], NB)
            a.activation(small[0:NP, 14, :], small[0:NP, 13, :], ACT.Copy, scale=-1.0 / D) \
                .then_inc(s["x_summed"], 1)
            act.wait_ge(s["x_summed"], NB + 1)
            for b in range(NB):
                wait(act, "x_squared", b - 1)
                a.activation(square_out[0:NP, b % 2, :], xin[:, b, :], ACT.Square, bias=small[0:NP, 14, b:b + 1],
                             accum_out=small[0:NP, 0, b:b + 1]).then_inc(s["x_squared"], 1)
            act.wait_ge(s["var_ready"], 1)
            a.activation(small[0:NP, 1, :], small[0:NP, 0, :], ACT.Sqrt).then_inc(s["std_ready"], 1)
            for b in range(NB):
                wait(act, "x_squared", NB if b == 0 else 0)
                a.activation(xin[:, b, :], xin[:, b, :], ACT.Identity, bias=small[0:NP, 14, b:b + 1]) \
                    .then_inc(s["x_centred"], 1)
            act.wait_ge(s["rstd_ready"], 1)
            for b in range(NB):
                act.wait_ge(s["x_centred"], b + 1)
                a.activation(h[:, b, :], xin[:, b, :], ACT.Relu, scale=small[0:NP, 3, b:b + 1]) \
                    .then_inc(s["h_ready"], 1)
            for b in range(NB):
                act.wait_ge(s["h_ready"], b + 1)
                wait(act, "sq_setup", b - 1)
                a.activation(square_out[0:NP, b % 2, 0:D - 1], h[:, b, 1:D], ACT.Square,
                             accum_out=small[0:NP, 2, b:b + 1]).then_inc(s["sq_setup"], 1)
            act.wait_ge(s["theta_ready"], 1)
            act.wait_ge(s["sq_setup"], NB)
            a.activation(small[0:NP, 6, :], small[0:NP, 5, :], ACT.Sqrt).then_inc(s["root_ready"], 1)
            a.activation(small[0:NP, 7, :], small[0:NP, 2, :], ACT.Sqrt).then_inc(s["root_ready"], 1)
            act.wait_ge(s["log_arg"], 1)
            a.activation(small[0:NP, 9, :], small[0:NP, 8, :], ACT.Ln).then_inc(s["log_ready"], 1)
            act.wait_ge(s["coef_ready"], 1)
            act.wait_ge(s["sort_done"], 1)
            def scale_column(c, slot, first_use=False):
                if not first_use:
                    act.wait_ge(s["hots_used"], c + (1 - HOT))
                act.wait_ge(s["hots_built"], c * 4 + 1)
                for k in range(2, 6):
                    part = (*word_parts, *dist_terms)[k]
                    a.activation(slot_val[0:NP, slot, k, :], slot_hot[0:NP, slot, :], ACT.Copy,
                                 scale=part[:, bass.ds(c + (EC - MOVED), 1)]).then_inc(s["hots_scaled"], 1)

            def copy_turn(b):
                act.wait_ge(s["ht_ps"], b + 1)
                wait(act, "pq_ps", b - 1)
                a.activation(hT[:, b % 2, 0:2 * NP], turn_ps[b % 2][:, 0:2 * NP], ACT.Copy).then_inc(s["ht_sb"], 1)

            def second_part(b):
                act.wait_ge(s["rest_ready"], 2 * b + 2)
                a.activation(parts[1][0:NP, b, :].rearrange("p (a d) -> p a d", a=2), rest[0:NP, :, :], ACT.Copy) \
                    .then_inc(s["part1"], 1)

            def self_square(b):
                act.wait_ge(s["self_u"], b + 1)
                wait(act, "self_sq", b - 1)
                a.activation(square_out[0:NP, b % 2, 0:D - 1], self_u[:, b % 2, 1:D], ACT.Square,
                             accum_out=small[0:NP, 17, b:b + 1]).then_inc(s["self_sq"], 1)

            copy_turn(0)
            for b in range(NB):
                if b + 1 < NB:
                    copy_turn(b + 1)
                a.activation(parts[0][0:NP, b, 0:D], h[:, b, :], ACT.Copy).then_inc(s["part0"], 1)
                if b:
                    second_part(b - 1)
                act.wait_ge(s["pq_ps"], b + 1)
                wait(act, "rest_ready", 2 * (b - 1))
                a.activation(pf[0:NP, b % 2, :], z_ps[b % 2][0:NP, 0:D], ACT.Copy,
                             scale=small[0:NP, 11, b:b + 1]).then_inc(s["pf_ready"], 1)
                act.wait_ge(s["pf_ready"], b + 1)
                a.activation(parts[0][0:NP, b, D:2 * D], pf[0:NP, b % 2, :], ACT.Copy).then_inc(s["part0"], 1)
                if b:
                    self_square(b - 1)
            second_part(NB - 1)
            self_square(NB - 1)
            act.wait_ge(s["part2"], NB)
            for slot in range(HOT):
                scale_column(slot, slot, first_use=True)
            with act.Fori(1, MOVED // HOT) as i:
                for slot in range(HOT):
                    scale_column(i * HOT + slot, slot)

            n_said = [0]

            def say(o, i, f, scale=1.0, cols=range(NB)):
                n_said[0] += 1
                act.wait_ge(s["tail_ask"], n_said[0])
                a.activation(small[0:NP, o, cols.start:cols.stop], small[0:NP, i, cols.start:cols.stop], f,
                             scale=scale).then_inc(s["tail_say"], 1)

            say(20, 19, ACT.Sqrt, -1.0)
            say(22, 21, ACT.Ln)
            say(20, 19, ACT.Sqrt)

            def copy_turned(gr, j):
                slot = j % 2
                wait(act, "at_ready", at(gr, PG, j + 1))
                wait(act, "expanded", at(gr, PG, j - 1))
                a.activation(onehot_t[:, slot, :, :].rearrange("p k e -> p (k e)"), at_ps[slot], ACT.Copy) \
                    .then_inc(s["at_copied"], 1)

            def hidden_layer(gr, j):
                slot = j % 2
                wait(act, "expanded", at(gr, PG, j + 1))
                wait(act, "dot_done", at(gr, TG, 2 * j - 2))
                a.activation(hidden[:, slot, :, :], two(z_ps[slot]), ACT.Silu) \
                    .then_inc(s["silu_done"], 1)

            def square_tangents(gr, j):
                if not there(gr):
                    return
                par = gr[1] % 2
                for k in range(2):
                    wait(act, "u_ready", at(gr, TG, 2 * j + k + 1))
                    wait(act, "sq_done", at(gr, TG, 2 * j + k - 1))
                    a.activation(square_out[:, k, 0:D - 1], tangents[:, par, 2 * j + k, 1:D], ACT.Square,
                                 accum_out=uu[:, par, 2 * j + k:2 * j + k + 1]).then_inc(s["sq_done"], 1)

            def roots(gr):
                if not there(gr):
                    return
                asks = (
                    (3, wt[2], wt[1], ACT.Ln, -1.0, 0.0),
                    (3, wt[3], wt[2], ACT.Exp, 0.5, 0.0),
                    (5, wt[4], wt[8], ACT.Ln, 1.0, 0.0),
                    (5, wt[6], wt[4], ACT.Exp, -0.5, 0.0),
                    (5, wt[9], logit[:, gr[1] % 2, :], ACT.Exp, -1.0, nb2col[:, :]),
                    (6, wt[10], wt[5], ACT.Ln, 1.0, 0.0))
                a.preload_act_table_set("natural_log_exp_and_others")
                wait(act, "dot_done", at(gr, TG, TG))
                for n, (after, o, i, f, scale, bias) in enumerate(asks):
                    wait(act, "w_vec", at(gr, CHAIN, after))
                    if n in (1, 3):
                        wait(act, "w_act", at(gr, CHAIN_A, n))
                    a.activation(o[:, :], i if n == 4 else i[:, :], f, scale=scale, bias=bias).then_inc(s["w_act"], 1)

            def weigh_onehots(gr, j):
                if not there(gr):
                    return
                slot, par = j % 2, gr[1] % 2
                wait(act, "w_vec", at(gr, CHAIN, CHAIN))
                wait(act, "agg_summed", at(gr, PG, j - 1))
                for k in range(2):
                    a.activation(weighted[:, slot, k, 0:NP], onehot[:, par * TG + 2 * j + k, 0:NP], ACT.Copy,
                                 scale=weight[:, par, 2 * j + k:2 * j + k + 1]).then_inc(s["weighted_ready"], 1)

            def act_group(gr):
                for j in range(PG):
                    weigh_onehots(*pair(gr, j, -LAG))
                    hidden_layer(gr, j)
                    copy_turned(*pair(gr, j, 2))
                    square_tangents(*pair(gr, j, -1))
                    if j == 1:
                        roots((gr[0], gr[1] - 1))

            act.wait_ge(s["sort_over"], 1)
            a.activation(sums[:, :, :], ones[:, None, 0:1].broadcast_to((P, NB, D)), ACT.Copy, scale=0.0) \
                .then_inc(s["sums_zero"], 1)
            copy_turned((0, 0), 0)
            copy_turned((0, 0), 1)
            groups(act, act_group)
            square_tangents((0, NG - 1), PG - 1)
            roots((0, NG - 1))
            pairs_left(weigh_onehots, LAG)

            def square_outs(q):
                for b in quad(q):
                    act.wait_ge(s["o_ready"], b + 1)
                    wait(act, "o_sq", b - 1)
                    a.activation(square_out[0:NP, b % 2, 0:D - 1], sums[0:NP, b, 1:D], ACT.Square,
                                 accum_out=small[0:NP, 18, b:b + 1]).then_inc(s["o_sq"], 1)

            act.wait_ge(s["sq_done"], J)
            for q in range(NQ):
                n_cols = len(quad(q)) * NP
                act.wait_ge(s["t_ps"], q + 1)
                wait(act, "m1_ps", 2 * (q - 1))
                for c in range(2):
                    a.activation(sumT[q % 2][:, c, 0:n_cols], turn_ps[c][:, 0:n_cols], ACT.Copy, scale=0.01) \
                        .then_inc(s["t_sb"], 1)
                for f in range(2):
                    act.wait_ge(s["m1_ps"], 2 * q + f + 1)
                    wait(act, "m2_ps", 4 * (q - 1))
                    a.activation(hidT[q % 2][:, f, 0:n_cols], z_ps[f][:, 0:n_cols], ACT.Silu,
                                 bias=mb1col[:, f:f + 1]).then_inc(s["m1_sb"], 1)
                if q:
                    square_outs(q - 1)
            square_outs(NQ - 1)
            say(4, 3, ACT.Sqrt)
            say(5, 4, ACT.Exp)
            say(6, 4, ACT.Exp, -1.0)
            n_y = [0]

            def square_ys(chunk):
                for b in order(chunk):
                    if b % 2:
                        a.activation(sums[0:NP, b, :], sums[0:NP, b, :], ACT.Copy, scale=small[0:NP, 8, b:b + 1]) \
                            .then_inc(s["y_scaled"], 1)
                for b in order(chunk):
                    n_y[0] += 1
                    act.wait_ge(s["y_ready"], n_y[0])
                    wait(act, "y_sq", n_y[0] - 2)
                    a.activation(square_out[0:NP, n_y[0] % 2, 0:D - 1], sums[0:NP, b, 1:D], ACT.Square,
                                 accum_out=small[0:NP, 13, b:b + 1]).then_inc(s["y_sq"], 1)

            act.wait_ge(s["y_begin"], 1)
            act.wait_ge(s["o_sq"], NB)
            for n, chunk in enumerate(CHUNKS):
                square_ys(chunk)
                if n:
                    say(15, 14, ACT.Sqrt, cols=CHUNKS[n - 1])
            say(15, 14, ACT.Sqrt, cols=CHUNKS[-1])

        @block.vector
        def _(dve):
            v = nc.vector
            n = [0]

            def step(ins):
                n[0] += 1
                ins.then_inc(s["vec"], 1)
                dve.wait_ge(s["vec"], n[0])

            def mark(ins):
                n[0] += 1
                ins.then_inc(s["vec"], 1)
                return n[0]

            def sm(k, rows=NP):
                return small[0:rows, k, :]

            dve.wait_ge(s["edges_in"], 48)
            step(v.tensor_copy(src_f, src_i))
            step(v.tensor_scalar(buck, src_f, 1.0 / NP, 0.5 / NP - 0.5, ALU.mult, ALU.add))
            step(v.tensor_scalar(buck, buck, MAGIC, None, ALU.add))
            step(v.tensor_scalar(buck, buck, -MAGIC, None, ALU.add))
            step(v.scalar_tensor_tensor(local, buck, -float(NP), src_f, ALU.mult, ALU.add))
            for b in range(NB):
                mark(v.tensor_scalar(inds[b], buck, float(b), None, ALU.is_equal, ALU.add,
                                     accum_out=counts[0:NP, b:b + 1]))
            dve.wait_ge(s["vec"], n[0])
            dve.nop().then_inc(s["counted"], 1)
            step(v.memset(ones_row, 1.0))
            step(v.tensor_copy(dst_f, dst_i))
            step(v.tensor_scalar(word_parts[0], local, float(WORD), float(WORD), ALU.mult, ALU.add))
            step(v.tensor_tensor(rec_src[:, :, 0], word_parts[0], dst_f, ALU.add))
            step(v.tensor_copy(rec_src[:, :, 1], dist_in))
            dve.wait_ge(s["consts_ready"], 1)
            dve.wait_ge(s["count_ps"], 1)
            step(v.tensor_scalar(off[:, 0, :], agg_ps[1][:, 0:NB], 1.0 / PAIR, (PAIR - 1.0) / PAIR - 0.498,
                                 ALU.mult, ALU.add))
            step(v.tensor_scalar(off[:, 0, :], off[:, 0, :], MAGIC, None, ALU.add))
            step(v.tensor_scalar(off[:, 0, :], off[:, 0, :], -MAGIC, None, ALU.add))
            step(v.tensor_tensor_scan(off[:, 1, :], ones[:, 0:NB], off[:, 0, :], 0.0, ALU.mult, ALU.add))
            step(v.tensor_tensor(off[:, 2, :], off[:, 1, :], off[:, 0, :], ALU.subtract))
            step(v.scalar_tensor_tensor(off[0:NP, 3, :], off[0:NP, 2, :], float(PAIR), agg_ps[0][0:NP, 0:NB],
                                        ALU.mult, ALU.add))
            step(v.tensor_scalar(off[0:NP, 4, :], off[0:NP, 3, :], -1.0, None, ALU.add))
            dve.nop().then_inc(s["base_done"], 1)
            def rank(b):
                return mark(v.tensor_tensor_scan(scans[b % 3], ones_row, inds[b], off[0:NP, 4, b:b + 1],
                                                 ALU.mult, ALU.add))

            ranked, picked = rank(0), 0
            for b in range(NB + 1):
                ranks, ranked = ranked, rank(b + 1) if b + 1 < NB else 0
                if b:
                    dve.wait_ge(s["vec"], picked)
                if b > 1:
                    mark(v.tensor_tensor(pos, pos, picks[(b - 1) % 2], ALU.add))
                if b < NB:
                    dve.wait_ge(s["vec"], ranks)
                    picked = mark(v.tensor_tensor(pos if b == 0 else picks[b % 2], inds[b], scans[b % 3], ALU.mult))
                if b == NB - 8:
                    dve.wait_ge(s["x_squared"], NB)
                    v.tensor_scalar(sm(0), sm(0), 1.0 / D, 1e-5, ALU.mult, ALU.add).then_inc(s["var_ready"], 1)
                if b == NB - 4:
                    dve.wait_ge(s["std_ready"], 1)
                    v.reciprocal(sm(3), sm(1)).then_inc(s["rstd_ready"], 1)
            dve.wait_ge(s["vec"], n[0])
            step(v.tensor_copy(pos_i, pos))
            step(v.tensor_scalar(lo_i, pos_i, P - 1, None, ALU.bitwise_and))
            step(v.tensor_scalar(hi_i, pos_i, P.bit_length() - 1, None, ALU.logical_shift_right))
            step(v.tensor_copy(src_f, lo_i))
            step(v.tensor_copy(tmp, hi_i))
            step(v.scalar_tensor_tensor(pos, src_f, float(J), tmp, ALU.mult, ALU.add))
            step(v.tensor_copy(row_i, pos))
            dve.nop().then_inc(s["sort_done"], 1)
            dve.wait_ge(s["weights_in"], 16 * 9)
            step(v.tensor_scalar(nb2col[:, :], b2col[:, :], -1.0, None, ALU.mult))
            step(v.tensor_copy(w1c_parts[:, 0, :], w1c[:, :]))
            step(v.tensor_tensor(w1c[:, :], w1c[:, :], w1c_parts[:, 0, :], ALU.subtract))
            step(v.tensor_copy(w1c_parts[:, 1, :], w1c[:, :]))
            step(v.tensor_tensor(w1c_parts[:, 2, :], w1c[:, :], w1c_parts[:, 1, :], ALU.subtract))
            dve.nop().then_inc(s["w1c_split"], 1)

            dve.wait_ge(s["h_ready"], NB)
            step(v.tensor_scalar(sm(3), h[:, :, 0], 1.0 + EPS, None, ALU.max))
            step(v.tensor_scalar(sm(4), sm(3), -1.0, None, ALU.add))
            step(v.scalar_tensor_tensor(sm(5), sm(3), 1.0, sm(4), ALU.add, ALU.mult))
            dve.nop().then_inc(s["theta_ready"], 1)
            dve.wait_ge(s["root_ready"], 2)
            step(v.tensor_tensor(sm(8), sm(6), sm(3), ALU.add))
            dve.nop().then_inc(s["log_arg"], 1)
            step(v.tensor_scalar(sm(7), sm(7), 1e-15, None, ALU.max))
            step(v.reciprocal(sm(10), sm(7)))
            dve.wait_ge(s["log_ready"], 1)
            step(v.tensor_tensor(sm(11), sm(9), sm(10), ALU.mult))
            dve.nop().then_inc(s["coef_ready"], 1)
            step(v.tensor_tensor(sm(12), h[:, :, 0], h[:, :, 0], ALU.mult))
            step(v.tensor_tensor(sm(12), sm(2), sm(12), ALU.subtract))
            step(v.tensor_scalar(sm(12), sm(12), SELF_MAX, None, ALU.min))
            shift = LOW.bit_length() - 1
            step(v.tensor_scalar(lo_i, dst_i, shift, None, ALU.logical_shift_right))
            step(v.tensor_scalar(lo_i, lo_i, shift, None, ALU.logical_shift_left))
            step(v.tensor_copy(word_parts[1], lo_i))
            step(v.tensor_tensor(word_parts[2], dst_f, word_parts[1], ALU.subtract))
            step(v.tensor_copy(rough, dist_in))
            step(v.tensor_copy(dist_terms[0], rough))
            step(v.tensor_tensor(dist_terms[2], dist_in, dist_terms[0], ALU.subtract))
            step(v.tensor_copy(rough, dist_terms[2]))
            step(v.tensor_copy(dist_terms[1], rough))
            step(v.tensor_tensor(dist_terms[2], dist_terms[2], dist_terms[1], ALU.subtract))
            dve.wait_ge(s["tile_iota"], 1)

            def build_column(c, slot, first_use=False):
                here = bass.ds(c + (EC - MOVED), 1)
                if not first_use:
                    dve.wait_ge(s["hots_used"], c + (1 - HOT))
                v.tensor_scalar(slot_hot[0:NP, slot, :], iota_b[0:NP, :], slot_f[:, here], None,
                                ALU.is_equal).then_inc(s["hots_built"], 1)
                v.tensor_scalar(tile_hot[0:NP, slot, :], tile_iota[0:NP, :], tile_f[:, here], None,
                                ALU.is_equal).then_inc(s["hots_built"], 1)
                for k in range(2):
                    v.tensor_scalar(slot_val[0:NP, slot, k, :], iota_b[0:NP, :], slot_f[:, here],
                                    word_parts[k][:, here], ALU.is_equal, ALU.mult).then_inc(s["hots_built"], 1)

            def third_part(b):
                dve.wait_ge(s["part1"], b + 1)
                v.tensor_tensor(parts[2][0:NP, b, :].rearrange("p (a d) -> p a d", a=2), rest[0:NP, :, :],
                                parts[1][0:NP, b, :].rearrange("p (a d) -> p a d", a=2),
                                ALU.subtract).then_inc(s["part2"], 1)

            step(v.memset(pair_acc[:, :], 0.0))
            for b in range(NB):
                if b:
                    third_part(b - 1)
                dve.wait_ge(s["part0"], 2 * b + 1)
                wait(dve, "part2", b)
                v.tensor_tensor(rest[0:NP, 0, :], h[:, b, :], parts[0][0:NP, b, 0:D], ALU.subtract) \
                    .then_inc(s["rest_ready"], 1)
                dve.wait_ge(s["part0"], 2 * b + 2)
                v.tensor_tensor(rest[0:NP, 1, :], pf[0:NP, b % 2, :], parts[0][0:NP, b, D:2 * D], ALU.subtract) \
                    .then_inc(s["rest_ready"], 1)
                dve.wait_ge(s["pq_ps"], b + 1)
                v.scalar_tensor_tensor(xin[:, b, :], h_ps[b % 2][0:NP, 0:D], small[0:NP, 11, b:b + 1],
                                       b1row[0:NP, :], ALU.mult, ALU.add).then_inc(s["q_ready"], 1)
                wait(dve, "self_sq", b - 1)
                v.scalar_tensor_tensor(self_u[:, b % 2, :], h[:, b, :], small[0:NP, 12, b:b + 1], h[:, b, :],
                                       ALU.mult, ALU.add).then_inc(s["self_u"], 1)
                if b < NB - 1:
                    dve.wait_ge(s["vec"], n[0])
                    mark(v.scalar_tensor_tensor(pair_acc[:, :], pair_iota[:, :], off[0:1, 1, b:b + 1],
                                                pair_acc[:, :], ALU.is_ge, ALU.add))
            dve.wait_ge(s["vec"], n[0])
            third_part(NB - 1)
            dve.wait_ge(s["part2"], NB)
            dve.wait_ge(s["table_tails"], 48)
            for slot in range(HOT):
                build_column(slot, slot, first_use=True)
            with dve.Fori(1, MOVED // HOT) as i:
                for slot in range(HOT):
                    build_column(i * HOT + slot, slot)
            step(v.tensor_copy(bucket_of[:, 0:NPAIR], pair_acc[:, :]))
            step(v.memset(bucket_of[:, NPAIR:NPAIR + 1], 0))
            dve.nop().then_inc(s["buckets_ready"], 1)

            asked = [0]

            def ask():
                asked[0] += 1
                dve.nop().then_inc(s["tail_ask"], 1)
                dve.wait_ge(s["tail_say"], asked[0])

            step(v.tensor_scalar(sm(14), h[:, :, 0], EPS, None, ALU.max))
            step(v.reciprocal(sm(0), sm(14)))
            dve.wait_ge(s["self_sq"], NB)
            step(v.tensor_tensor(sm(1), h[:, :, 0], sm(12), ALU.mult))
            step(v.tensor_tensor(sm(1), sm(1), h[:, :, 0], ALU.add))
            step(v.tensor_tensor(sm(1), sm(1), sm(1), ALU.mult))
            step(v.tensor_tensor(sm(2), sm(17), sm(1), ALU.subtract))
            step(v.tensor_scalar(sm(2), sm(2), EPS, None, ALU.max))
            step(v.reciprocal(sm(3), sm(2)))
            step(v.tensor_scalar(sm(4), sm(12), -1.0, -1.0, ALU.mult, ALU.add))
            step(v.scalar_tensor_tensor(sm(19), sm(12), 1.0, sm(4), ALU.subtract, ALU.mult))
            ask()
            step(v.tensor_tensor(sm(21), sm(20), sm(12), ALU.subtract))
            ask()
            step(v.tensor_tensor(sm(5), sm(22), sm(22), ALU.mult))
            step(v.scalar_tensor_tensor(sm(19), sm(5), 50.0, sm(3), ALU.min, ALU.mult))
            ask()
            dve.nop().then_inc(s["h_used"], 1)
            dve.wait_ge(s["recs_in"], 16)
            dve.wait_ge(s["hots_used"], MOVED)
            step(v.tensor_tensor(word, raw[:, :, 0], agg_ps[0][:, 0:J], ALU.add))
            step(v.tensor_copy(word_i, word))
            step(v.tensor_scalar(recs[:, 0:J, 1].bitcast(i32), word_i, WORD - 1, None, ALU.bitwise_and))
            step(v.tensor_scalar(high_i, word_i, WORD.bit_length() - 1, None, ALU.logical_shift_right))
            step(v.tensor_copy(recs[:, 0:J, 0], high_i))
            step(v.memset(recs[:, J:, :], 0.0))
            dve.nop().then_inc(s["recs_ready"], 1)
            step(v.tensor_scalar(recs[:, :, 0], recs[:, :, 0], -1.0, None, ALU.add))
            step(v.tensor_tensor(recs[:, 0:J, 2], raw[:, :, 1], agg_ps[1][:, 0:J], ALU.add))
            dve.nop().then_inc(s["sort_over"], 1)
            step(v.tensor_copy(dist_parts[:, :, 0], recs[:, :, 2]))
            step(v.tensor_tensor(rest_d, recs[:, :, 2], dist_parts[:, :, 0], ALU.subtract))
            step(v.tensor_copy(dist_parts[:, :, 1], rest_d))
            step(v.tensor_tensor(dist_parts[:, :, 2], rest_d, dist_parts[:, :, 1], ALU.subtract))

            dve.nop().then_inc(s["agg_added"], 1)
            dve.nop().then_inc(s["agg_added"], 1)
            bucket = [v.alloc_register(f"dve_bucket{j}") for j in range(2)]

            def build_onehot(gr, j, k):
                ring = (gr[1] % 2) * TG + 2 * j
                wait(dve, "weighted_ready", at(gr, TG, 2 * j + 2 - 2 * TG))
                v.tensor_scalar(onehot[:, ring + k, 0:NP], iota_b[:, 0:NP],
                                recs[:, bass.ds(at(gr, TG, 2 * j + k), 1), 0], None,
                                ALU.is_equal).then_inc(s["onehots"], 1)

            def build_distance(gr, j):
                ring = (gr[1] % 2) * TG + 2 * j
                v.tensor_copy(onehot[:, ring:ring + 2, NP:P], dist_parts[:, bass.ds(at(gr, TG, 2 * j), 2), :]) \
                    .then_inc(s["onehots"], 1)

            def attention_dot(gr, j, k):
                if not there(gr):
                    return
                slot, par = j % 2, gr[1] % 2
                wait(dve, "silu_done", at(gr, PG, j + 1))
                wait(dve, "dot_done", at(gr, TG, 2 * j + k - 1))
                v.tensor_tensor_reduce(out=dot_out[:, k, :], in0=hidden[:, slot, k, :], in1=w2row[:, :],
                                       scale=1.0, scalar=0.0, op0=ALU.mult, op1=ALU.add,
                                       accum_out=logit[:, par, 2 * j + k:2 * j + k + 1]) \
                    .then_inc(s["dot_done"], 1)

            def load_bucket(gr, j):
                if there(gr):
                    v.reg_load(bucket[j % 2], bucket_of[0:1, bass.ds(at(gr, PG, j), 1)])

            def add_sums(gr, j):
                if not there(gr):
                    return
                b = v.snap(bucket[j % 2])
                wait(dve, "agg_summed", at(gr, PG, j + 1))
                wait(dve, "agg_added", at(gr, PG, j + 2))
                v.tensor_tensor(sums[0:NP, bass.ds(b, 1), :], agg_ps[j % 2][0:NP, None, 0:D],
                                sums[0:NP, bass.ds(b, 1), :], ALU.add).then_inc(s["agg_added"], 1)

            def vec_pair(gr, j, between):
                slot, par = j % 2, gr[1] % 2
                new, old = pair(gr, j, 3), pair(gr, j, -1)
                build_onehot(*new, 0)
                wait(dve, "expanded", at(gr, PG, j + 1))
                v.scalar_tensor_tensor(neg0[:, slot, :], two(h_ps[slot])[:, :, 0], -1.0,
                                       gathered[:, j, :, 0], ALU.mult, ALU.mult).then_inc(s["neg_done"], 1)
                build_onehot(*new, 1)
                build_distance(*new)
                between(0)
                attention_dot(*old, 0)
                wait(dve, "neg_done", at(gr, PG, j + 1))
                for k in range(2):
                    wait(dve, "mink_done", at(gr, TG, 2 * j + k - 1))
                    v.tensor_tensor_reduce(out=mink_out[:, k, 0:D - 1], in0=h_ps[slot][:, k * D + 1:(k + 1) * D],
                                           in1=gathered[:, j, k, 1:D], scale=1.0,
                                           scalar=neg0[:, slot, k:k + 1], op0=ALU.mult, op1=ALU.add,
                                           accum_out=mink[:, 2 * j + k:2 * j + k + 1]).then_inc(s["mink_done"], 1)
                between(1)
                add_sums(*pair(gr, j, -LAG - 2))
                wait(dve, "mink_done", at(gr, TG, 2 * j + 2))
                v.tensor_scalar(xy[:, par, 2 * j:2 * j + 2], mink[:, 2 * j:2 * j + 2], SELF_MAX, None,
                                ALU.min).then_inc(s["xy_done"], 1)
                between(2)
                attention_dot(*old, 1)
                wait(dve, "xy_done", at(gr, PG, j + 1))
                for k in range(2):
                    v.scalar_tensor_tensor(tangents[:, par, 2 * j + k, :], h_ps[slot][:, k * D:(k + 1) * D],
                                           xy[:, par, 2 * j + k:2 * j + k + 1], gathered[:, j, k, 0:D],
                                           ALU.mult, ALU.add).then_inc(s["u_ready"], 1)
                between(3)

            PLACES = ((0, 0), (0, 1), (0, 2), (1, 0), (1, 1), (2, 0), (2, 1), (2, 2), (2, 3), (3, 0), (3, 1))
            assert len(PLACES) == CHAIN

            def to_weight(gr, step_no):
                if not there(gr):
                    return
                par = gr[1] % 2
                xys = xy[:, par, :]
                wait(dve, "w_vec", at(gr, CHAIN, step_no - 1))
                if step_no == 1:
                    ins = v.tensor_scalar(wt[0][:, :], xys, -1.0, -1.0, ALU.mult, ALU.add)
                elif step_no == 2:
                    ins = v.tensor_tensor(wt[7][:, :], tangents[:, par, :, 0], tangents[:, par, :, 0], ALU.mult)
                elif step_no == 3:
                    ins = v.scalar_tensor_tensor(wt[1][:, :], xys, 1.0, wt[0][:, :], ALU.subtract, ALU.mult)
                elif step_no == 4:
                    wait(dve, "sq_done", at(gr, TG, TG))
                    ins = v.tensor_tensor(wt[8][:, :], uu[:, par, :], wt[7][:, :], ALU.subtract)
                elif step_no == 5:
                    ins = v.tensor_scalar(wt[8][:, :], wt[8][:, :], EPS, None, ALU.max)
                elif step_no == 6:
                    wait(dve, "w_act", at(gr, CHAIN_A, 2))
                    ins = v.tensor_tensor(wt[5][:, :], wt[3][:, :], xys, ALU.subtract)
                elif step_no == 7:
                    wait(dve, "w_act", at(gr, CHAIN_A, 5))
                    ins = v.tensor_scalar(wt[11][:, :], wt[9][:, :], 1.0, None, ALU.add)
                elif step_no == 8:
                    ins = v.reciprocal(wt[12][:, :], wt[11][:, :])
                elif step_no == 9:
                    ins = v.tensor_tensor(wt[0][:, :], wt[12][:, :], recs[:, bass.ds(at(gr, TG, 0), TG), 2],
                                          ALU.mult)
                elif step_no == 10:
                    wait(dve, "w_act", at(gr, CHAIN_A, 6))
                    ins = v.scalar_tensor_tensor(wt[1][:, :], wt[10][:, :], ROOT50, wt[6][:, :],
                                                 ALU.min, ALU.mult)
                else:
                    ins = v.tensor_tensor(weight[:, par, :], wt[0][:, :], wt[1][:, :], ALU.mult)
                ins.then_inc(s["w_vec"], 1)

            def vec_group(gr):
                for j in range(PG):
                    def between(place):
                        if (j, place) in PLACES:
                            to_weight((gr[0], gr[1] - 1), PLACES.index((j, place)) + 1)

                    vec_pair(gr, j, between)
                    load_bucket(*pair(gr, j, -LAG - 1))

            for j in range(3):
                for k in range(2):
                    build_onehot((0, 0), j, k)
                build_distance((0, 0), j)
            dve.wait_ge(s["sums_zero"], 1)
            groups(dve, vec_group)
            add_sums(*pair((0, NG - 1), PG - 1, -LAG - 1))
            for k in range(2):
                attention_dot((0, NG - 1), PG - 1, k)
            for step_no in range(1, CHAIN + 1):
                to_weight((0, NG - 1), step_no)

            def last_sums(gr, j):
                load_bucket(gr, j)
                add_sums(gr, j)

            pairs_left(last_sums, LAG + 1)

            dve.wait_ge(s["h_back"], 16)
            dve.wait_ge(s["agg_added"], NPAIR + 2)

            def trail(ins):
                mark(ins)
                dve.wait_ge(s["vec"], n[0] - 1)

            def fix_component_0(q):
                b0, b1 = quad(q).start, quad(q).stop
                for b in quad(q):
                    trail(v.tensor_tensor_reduce(out=mink_out[0:NP, b % 2, 0:D - 1], in0=h[:, b, 1:D],
                                                 in1=sums[0:NP, b, 1:D], scale=1.0, scalar=0.0, op0=ALU.mult,
                                                 op1=ALU.add, accum_out=small[0:NP, 23, b:b + 1]))
                dve.wait_ge(s["vec"], n[0])
                step(v.tensor_tensor(sums[0:NP, b0:b1, 0], small[0:NP, 23, b0:b1], small[0:NP, 0, b0:b1], ALU.mult))
                dve.nop().then_inc(s["tail_agg"], 1)

            def self_logmap(q):
                for b in quad(q):
                    mark(v.scalar_tensor_tensor(self_tangents[:, b, :], h[:, b, :], small[0:NP, 12, b:b + 1],
                                                h[:, b, :], ALU.mult, ALU.add))
                dve.wait_ge(s["vec"], n[0])
                for b in quad(q):
                    mark(v.scalar_tensor_tensor(self_tangents[:, b, :], self_tangents[:, b, :],
                                                small[0:NP, 20, b:b + 1], mb2row[0:NP, :], ALU.mult, ALU.add))
                dve.wait_ge(s["vec"], n[0])

            def out_dot(b):
                dve.wait_ge(s["o_ready"], b + 1)
                wait(dve, "o_dot", b - 1)
                v.tensor_tensor_reduce(out=dot_out[0:NP, b % 2, 0:D - 1], in0=h[:, b, 1:D], in1=sums[0:NP, b, 1:D],
                                       scale=1.0, scalar=0.0, op0=ALU.mult, op1=ALU.add,
                                       accum_out=small[0:NP, 16, b:b + 1]).then_inc(s["o_dot"], 1)

            fix_component_0(0)
            fix_component_0(1)
            for q in range(NQ):
                self_logmap(q)
                if q + 2 < NQ:
                    fix_component_0(q + 2)
                for b in quad(q):
                    dve.wait_ge(s["m2_ps"], b + 1)
                    v.tensor_tensor(sums[0:NP, b, :], agg_ps[b % 2][0:NP, 0:D], self_tangents[:, b, :],
                                    ALU.add).then_inc(s["o_ready"], 1)
                    if b:
                        out_dot(b - 1)
            out_dot(NB - 1)
            dve.wait_ge(s["o_dot"], NB)
            dve.wait_ge(s["o_sq"], NB)
            step(v.tensor_tensor(sm(1), sm(16), sm(0), ALU.mult))
            step(v.tensor_tensor(sm(2), sm(1), sm(1), ALU.mult))
            step(v.tensor_tensor(sm(3), sm(18), sm(2), ALU.subtract))
            step(v.tensor_scalar(sm(3), sm(3), EPS, None, ALU.max))
            ask()
            step(v.tensor_scalar(sm(4), sm(4), 1e6, 1e-15, ALU.min, ALU.max))
            ask()
            ask()
            step(v.tensor_tensor(sm(7), sm(5), sm(6), ALU.add))
            step(v.tensor_scalar(sm(7), sm(7), 0.5, None, ALU.mult))
            step(v.tensor_tensor(sm(8), sm(5), sm(6), ALU.subtract))
            step(v.reciprocal(sm(9), sm(4)))
            step(v.scalar_tensor_tensor(sm(8), sm(8), 0.5, sm(9), ALU.mult, ALU.mult))
            step(v.tensor_tensor(sm(9), sm(4), sm(4), ALU.mult))
            step(v.tensor_scalar(sm(9), sm(9), 1.0, None, ALU.min))
            step(v.tensor_scalar(sm(10), sm(4), 1.0, None, ALU.is_lt))
            step(v.tensor_scalar(sm(11), sm(4), 1.0, None, ALU.is_ge))
            for o, terms in ((21, (90.0, 56.0, 30.0, 12.0, 2.0)), (22, (110.0, 72.0, 42.0, 20.0, 6.0))):
                step(v.tensor_scalar(sm(o), sm(9), 1.0 / terms[0], 1.0, ALU.mult, ALU.add))
                for term in terms[1:]:
                    step(v.tensor_tensor(sm(o), sm(o), sm(9), ALU.mult))
                    step(v.tensor_scalar(sm(o), sm(o), 1.0 / term, 1.0, ALU.mult, ALU.add))
            for e, o in ((7, 21), (8, 22)):
                step(v.tensor_tensor(sm(e), sm(e), sm(11), ALU.mult))
                step(v.tensor_tensor(sm(o), sm(o), sm(10), ALU.mult))
                step(v.tensor_tensor(sm(e), sm(e), sm(o), ALU.add))
            dve.nop().then_inc(s["y_begin"], 1)
            dve.wait_ge(s["x_back"], 16)
            odd = [0]

            def make_ys(chunk):
                for b in order(chunk):
                    if b % 2:
                        v.tensor_scalar(sums[0:NP, b - 1, :], sums[0:NP, b - 1, :], small[0:NP, 8, b - 1:b], None,
                                        ALU.mult).then_inc(s["y_even"], 1)
                        odd[0] += 1
                        dve.wait_ge(s["y_scaled"], odd[0])
                    else:
                        if b + 1 == chunk.stop:
                            v.tensor_scalar(sums[0:NP, b, :], sums[0:NP, b, :], small[0:NP, 8, b:b + 1], None,
                                            ALU.mult).then_inc(s["y_even"], 1)
                        dve.wait_ge(s["y_even"], b // 2 + 1)
                    v.scalar_tensor_tensor(sums[0:NP, b, :], h[:, b, :], small[0:NP, 7, b:b + 1], sums[0:NP, b, :],
                                           ALU.mult, ALU.add).then_inc(s["y_ready"], 1)

            def finish(chunk):
                b0, b1 = chunk.start, chunk.stop
                dve.wait_ge(s["y_sq"], b1)
                step(v.tensor_scalar(small[0:NP, 14, b0:b1], small[0:NP, 13, b0:b1], 1.0, None, ALU.add))
                ask()
                step(v.tensor_copy(sums[0:NP, b0:b1, 0], small[0:NP, 15, b0:b1]))
                step(v.tensor_tensor(xin[:, b0:b1, :], xin[:, b0:b1, :], sums[0:NP, b0:b1, :], ALU.add))
                dve.nop().then_inc(s["out_ready"], 1)

            for n_chunk, chunk in enumerate(CHUNKS):
                make_ys(chunk)
                if n_chunk:
                    finish(CHUNKS[n_chunk - 1])
            finish(CHUNKS[-1])


_INS = ["x", "src", "dst", "edge_weight1", "L0_gnn_att_w1", "L0_gnn_att_b1", "L0_gnn_att_w2", "L0_gnn_att_b2",
        "L0_gnn_mlp_w1", "L0_gnn_mlp_b1", "L0_gnn_mlp_w2", "L0_gnn_mlp_b2"]


def kernel(**inputs):
    import numpy as _np
    import concourse.bacc as _bacc
    from concourse import mybir as _mybir
    from concourse.bass_utils import run_bass_kernel_spmd as _run

    nc = _bacc.Bacc("TRN2", target_bir_lowering=False, num_devices=1)
    arrays, args = {}, []
    for name in _INS:
        a = _np.ascontiguousarray(inputs[name])
        if name == "edge_weight1":
            a = a.reshape(-1)
        arrays[f"in_{name}_dram"] = a
        args.append(nc.dram_tensor(f"in_{name}_dram", a.shape, _mybir.dt.from_np(a.dtype), kind="ExternalInput").ap())
    shape = inputs["x"].shape
    args.append(nc.dram_tensor("out_0_dram", shape, _mybir.dt.from_np(_np.dtype("float32")),
                               kind="ExternalOutput").ap())
    hyperbolic_gnn_layer(nc, *args)
    r = _run(nc, [arrays], core_ids=[0])
    return r.results[0]["out_0_dram"]
```
